# Optimizing a Trainium2 kernel written in Bass

```python
import numpy as np
import jax
import jax.numpy as jnp

def _softmax(x, axis=-1):
    return jax.nn.softmax(x, axis=axis)

def _gelu(x):
    return jax.nn.gelu(x, approximate=True)

def _silu(x):
    return jax.nn.silu(x)

def _sigmoid(x):
    return jax.nn.sigmoid(x)

def _layernorm(x, axis=-1, eps=1e-05):
    m = jnp.mean(x, axis=axis, keepdims=True)
    v = jnp.var(x, axis=axis, keepdims=True)
    return (x - m) / jnp.sqrt(v + eps)

def _scatter_add(tgt, idx, src, axis=0):
    return tgt.at[idx].add(src)

def _segment_sum(src, seg, n):
    return jax.ops.segment_sum(src, seg, n)
kernel_name = 'mk_adj_resnorm_d2_adj_r2_2f5a1f'

def setup_inputs(seed: int=0):
    np.random.seed(seed)
    _w = jnp.asarray

    def _rec_inputs():
        import jax
        import jax.numpy as jnp
        _gk = jax.random.key(seed)
        x = -9.806e-05 + 1 * jax.random.normal(jax.random.fold_in(_gk, 1), (4096, 64), jnp.float32)
        _a = jax.random.bernoulli(jax.random.fold_in(_gk, 2), 0.000488281, (4096, 4096))
        _a = jnp.logical_or(_a, jnp.swapaxes(_a, -1, -2))
        _a = jnp.logical_or(_a, jnp.eye(4096, dtype=bool))
        adj = _a.astype(jnp.int32)
        return (x, adj)
    x, adj = _rec_inputs()

    def _L0_gnn_setup():
        import jax, jax.numpy as jnp
        import numpy as np
        N = 4096
        D = 64
        NEG_INF = -9000000000000000.0
        LEAKY_SLOPE = 0.01
        key = jax.random.key(seed)
        k1, k2, k3 = jax.random.split(key, 3)
        h = jax.random.normal(k1, (N, D), dtype=jnp.float32)
        adj = jax.random.randint(k2, (N, N), 0, 2, dtype=jnp.int32)
        bound = float(np.sqrt(6.0 / (2 * D + 1)))
        a = jax.random.uniform(k3, (2 * D, 1), dtype=jnp.float32, minval=-bound, maxval=bound)
        return {'h': h, 'adj': adj, 'a': a}
    _L0_gnn_all = _L0_gnn_setup()
    _L0_gnn_in = {k: v for k, v in _L0_gnn_all.items() if k in ('a',)}
    del _L0_gnn_all

    def _L1_gnn_setup():
        import jax, jax.numpy as jnp
        import numpy as np
        ALPHA = 0.2
        NEG_INF = -9000000000000000.0
        key = jax.random.key(seed)
        k1, k2, k3, k4 = jax.random.split(key, 4)
        N, F_IN, F_OUT = (512, 64, 64)
        h = jax.random.normal(k1, (N, F_IN), dtype=jnp.float32)
        adj = jax.random.randint(k2, (N, N), 0, 2, dtype=jnp.int32)
        lim_W = 1.414 * np.sqrt(6.0 / (F_IN + F_OUT))
        W = jax.random.uniform(k3, (F_IN, F_OUT), minval=-lim_W, maxval=lim_W, dtype=jnp.float32)
        lim_a = 1.414 * np.sqrt(6.0 / (2 * F_OUT + 1))
        a = jax.random.uniform(k4, (2 * F_OUT, 1), minval=-lim_a, maxval=lim_a, dtype=jnp.float32)
        return {'h': h, 'adj': adj, 'W': W, 'a': a}
    _L1_gnn_all = _L1_gnn_setup()
    _L1_gnn_in = {k: v for k, v in _L1_gnn_all.items() if k in ('W', 'a')}
    del _L1_gnn_all
    return {'x': x, 'adj': adj, 'L0_gnn_a': _L0_gnn_in['a'], 'L1_gnn_W': _L1_gnn_in['W'], 'L1_gnn_a': _L1_gnn_in['a']}

def reference(x, adj, L0_gnn_a, L1_gnn_W, L1_gnn_a):
    import jax
    import jax.numpy as jnp

    def _L0_gnn_ref(h, adj, a):
        import jax, jax.numpy as jnp
        import numpy as np
        N = 4096
        D = 64
        NEG_INF = -9000000000000000.0
        LEAKY_SLOPE = 0.01
        a1 = a[:D, 0]
        a2 = a[D:, 0]
        src = h @ a1
        dst = h @ a2
        e = src[:, None] + dst[None, :]
        e = jnp.where(e > 0, e, LEAKY_SLOPE * e)
        e = jnp.where(adj > 0, e, NEG_INF)
        attention = jax.nn.softmax(e, axis=1)
        h_prime = attention @ h
        return h_prime

    def _L1_gnn_ref(h, adj, W, a):
        import jax, jax.numpy as jnp
        import numpy as np
        ALPHA = 0.2
        NEG_INF = -9000000000000000.0
        F_OUT = W.shape[1]
        Wh = h @ W
        a1, a2 = (a[:F_OUT, 0], a[F_OUT:, 0])
        e = (Wh @ a1)[:, None] + (Wh @ a2)[None, :]
        e = jax.nn.leaky_relu(e, negative_slope=ALPHA)
        scores = jnp.where(adj > 0, e, jnp.float32(NEG_INF))
        attention = jax.nn.softmax(scores, axis=1)
        h_prime = attention @ Wh
        return jax.nn.elu(h_prime)
    x = _layernorm(x + _L0_gnn_ref(x, adj, L0_gnn_a), axis=-1)
    x = _layernorm(x + _L1_gnn_ref(x, adj, L1_gnn_W, L1_gnn_a), axis=-1)
    return x

_drawn_inputs = setup_inputs


def setup_inputs(seed=0):
    import zlib

    import numpy as np

    out = dict(_drawn_inputs(seed))
    spreads = {}
    factors = {}
    for name, (base, spread) in spreads.items():
        noise = np.random.default_rng([zlib.crc32(name.encode()), seed]).standard_normal(out[name].shape)
        drawn = base * np.exp(spread * noise) if base else spread * noise
        out[name] = jnp.asarray(drawn.astype(out[name].dtype))
    for name, factor in factors.items():
        out[name] = (out[name] * factor).astype(out[name].dtype)
    return out
```

```python
from contextlib import ExitStack

import concourse.bass as bass
from concourse import mybir

P = 128
N = 4096
F = 64
NQ = 8
TI = 4
KB = 8
NB = 4
ROWS = TI * P
HALF = N // 2
FD = F + 1
SPLIT = 3
WC = SPLIT * FD
SR = 4
MR = 2
SLOPE = (0.01, 0.2)
EPS = 1e-5
STEPS = NQ * KB
EPI = (13, 17)

ALU = mybir.AluOpType
ACT = mybir.ActivationFunctionType
AX = mybir.AxisListType
F32 = mybir.dt.float32
BF16 = mybir.dt.bfloat16
FP8 = mybir.dt.float8e4
I32 = mybir.dt.int32
U32 = mybir.dt.uint32
U16 = mybir.dt.uint16
U8 = mybir.dt.uint8
I8 = mybir.dt.int8


def fast_attention(nc, x, adj, a0, w1, a1, x1_dram, out):
    with ExitStack() as ctx:
        def sb(name, shape, dt):
            return ctx.enter_context(nc.sbuf_tensor(name, shape, dt))

        def ps(name, shape, dt):
            return ctx.enter_context(nc.psum_tensor(name, shape, dt))

        def sem(name):
            return ctx.enter_context(nc.semaphore(name))

        mask_t = sb("mask_t", [P, NQ, KB, TI, P], U32)
        adj_in = sb("adj_in", [P, 2, HALF], I32)
        enc = sb("enc", [P, 2, HALF // NB], F32)
        neg = sb("neg", [P, SR, ROWS, NB], I8)
        pos = sb("pos", [P, MR, ROWS, NB], I8)
        wmov = sb("wmov", [P, KB * NB, 2, SPLIT, FD], BF16)
        val = sb("val", [P, KB * NB, FD], F32)
        xt_s8 = sb("xt_s8", [P, ROWS], F32)
        scr = sb("scr", [P, 2, 2 * TI * FD], F32)
        resid = sb("resid", [P, TI, F], F32)
        xout = sb("xout", [P, TI, F], F32)
        ident = sb("ident", [P, P], F32)
        ones = sb("ones", [P, P], F32)
        pick = sb("pick", [P, P], F32)
        notid = sb("notid", [P, NQ], F32)
        att = sb("att", [F, 2, 2], F32)
        wl1 = sb("wl1", [F, 2 * F], F32)
        proj = sb("proj", [F, 2, F + 2], F32)
        selall = sb("selall", [F, 2, NQ * NQ], F32)
        selq = sb("selq", [F, NQ], F32)
        dcol = sb("dcol", [P, 2, KB * NB], F32)
        dcen = sb("dcen", [P, KB * NB], F32)
        scol = sb("scol", [P, NQ * TI], F32)
        scen = sb("scen", [P, 2, NQ * TI], F32)
        bcol = sb("bcol", [P, 2, KB * NB], F32)
        acol = sb("acol", [P, 2, NQ, TI], F32)
        stat = sb("stat", [P, 2], F32)
        gst = sb("gst", [2, 4], F32)
        cmax = sb("cmax", [P, 2], F32)
        meanv = sb("meanv", [P, F], F32)
        small = sb("small", [P, 6, TI], F32)
        bst = sb("bst", [P, TI, 6], F32)
        mv = sb("mv", [P, TI, 2], F32)

        xt = xt_s8[0:F, :]
        s8 = xt_s8[F:F + NQ, :]
        x_all = mask_t[:, NQ - 1, :, :, :].rearrange("p k t i -> p (k t i)")[:, 0:NQ * TI * F].bitcast(F32)\
            .rearrange("p (t d) -> p t d", d=F)

        acc = [ps(f"acc{t}", [P, 512], F32) for t in range(TI)]
        tb = [ps(f"tb{i}", [P, 4, P], F32) for i in range(2)]
        pg = ps("pg", [P, 512], F32)
        srcb = ps("srcb", [P, 512], F32)

        x_landed = sem("x_landed")
        w_landed = sem("w_landed")
        adj_landed = [sem(f"adj_landed{i}") for i in range(2)]
        res_landed = sem("res_landed")
        stored = sem("stored")
        ones_set = sem("ones_set")
        ident_zero = sem("ident_zero")
        ident_set = sem("ident_set")
        pdone = [sem(f"pdone{i}") for i in range(2)]
        consts = sem("consts")
        wt_turned = sem("wt_turned")
        wt_copied = sem("wt_copied")
        wa_ready = sem("wa_ready")
        encoded = sem("encoded")
        turned = sem("turned")
        masked = sem("masked")
        grp_turned = sem("grp_turned")
        xt_set = sem("xt_set")
        grp_proj = sem("grp_proj")
        grp_val = sem("grp_val")
        sel_set = sem("sel_set")
        grp_row = sem("grp_row")
        s8_set = sem("s8_set")
        picked = sem("picked")
        srcb_set = sem("srcb_set")
        stat_set = sem("stat_set")
        stat_turned = sem("stat_turned")
        gst_set = sem("gst_set")
        max_spread = sem("max_spread")
        cmax_set = sem("cmax_set")
        centred = sem("centred")
        exps = sem("exps")
        w_vec = sem("w_vec")
        w_act = sem("w_act")
        mean_sum = sem("mean_sum")
        mean_ps = sem("mean_ps")
        mean_set = sem("mean_set")
        signs = sem("signs")
        negs = sem("negs")
        poss = sem("poss")
        mm_done = sem("mm_done")
        acc_ready = sem("acc_ready")
        acc_free = sem("acc_free")
        recips = sem("recips")
        bn_part = sem("bn_part")
        bn_done = sem("bn_done")
        elu_exp = sem("elu_exp")

        adj_v = adj.rearrange("(q t p) (h j) -> q t h p j", t=TI, p=P, h=2)
        x_v = x.rearrange("(q t p) d -> q p t d", t=TI, p=P)
        x1_v = x1_dram.rearrange("(q t p) d -> q p t d", t=TI, p=P)
        out_v = out.rearrange("(q t p) d -> q p t d", t=TI, p=P)

        neg16 = neg[:, :, :, :].rearrange("p r i b -> p r (i b)").bitcast(U16)
        pos16 = pos[:, :, :, :].rearrange("p r i b -> p r (i b)").bitcast(U16)
        neg8 = neg[:, :, :, :].bitcast(FP8)
        pos8 = pos[:, :, :, :].bitcast(FP8)
        enc8 = enc[:, :, :].bitcast(FP8)
        part = scr[:, 0, :].rearrange("p (t s c) -> p t s c", t=TI, s=2)
        num = scr[:, 1, 0:TI * FD].rearrange("p (t c) -> p t c", t=TI)
        tmp = scr[:, 1, TI * FD:2 * TI * FD].rearrange("p (t c) -> p t c", t=TI)
        zero_row, den, rden, var, rstd, mhalf = (small[:, i, :] for i in range(6))

        def wide(col, c):
            return col.unsqueeze(2).broadcast_to([P, TI, c])

        def later(count):
            return not isinstance(count, int) or count > 0

        def apart(eng, count):
            if not isinstance(count, int):
                eng.nop(nofuse=True)

        def all_supertiles(eng, body, between):
            body(0, 0, True, False)
            with eng.Fori(1, NQ - 1) as q:
                body(0, q, True, True)
            body(0, NQ - 1, False, True)
            between()
            body(1, 0, False, False)
            with eng.Fori(1, NQ) as q:
                body(1, q, False, True)

        block = ctx.enter_context(nc.Block())

        @block.sync
        def _(sp):
            sp.dma_start(x_all, x.rearrange("(t p) d -> p t d", p=P)).then_inc(x_landed, 16)
            for half in range(2):
                sp.dma_start(att[:, 0, half:half + 1], a0[half * F:(half + 1) * F, :]).then_inc(w_landed, 16)
            for half in range(2):
                sp.dma_start(att[:, 1, half:half + 1], a1[half * F:(half + 1) * F, :]).then_inc(w_landed, 16)
            sp.dma_start(wl1[:, 0:F], w1).then_inc(w_landed, 16)

            def load_adj(q, k):
                if later(KB * q + k - 1):
                    sp.wait_ge(encoded, KB * q + k - 1)
                sp.dma_start(adj_in[:, k % 2, :], adj_v[q, k // 2, k % 2]).then_inc(adj_landed[k % 2], 16)

            def store(layer, q):
                sp.wait_ge(pdone[layer], EPI[layer] * (q + 1))
                sp.dma_start((x1_v if layer == 0 else out_v)[q], xout[:, :, :]).then_inc(stored, 16)

            def load_resid(layer, q):
                if layer == 1:
                    sp.wait_ge(stored, 16 * NQ)
                sp.dma_start(resid[:, :, :], (x_v if layer == 0 else x1_v)[q]).then_inc(res_landed, 16)

            def body(layer, q, prep, epi):
                for k in range(KB):
                    if prep:
                        load_adj(q + 1, k)
                if epi:
                    store(layer, q - 1)
                load_resid(layer, q)

            for k in range(KB):
                load_adj(0, k)
            all_supertiles(sp, body, lambda: store(0, NQ - 1))
            store(1, NQ - 1)
            sp.wait_ge(stored, 16 * 2 * NQ)

        @block.gpsimd
        def _(pool):
            nc.gpsimd.memset(ones[:, :], 1.0).then_inc(ones_set, 1)
            nc.gpsimd.memset(mhalf, -0.5).then_inc(ones_set, 1)
            nc.gpsimd.memset(ident[:, :], 0.0).then_inc(ident_zero, 1)
            pool.wait_ge(ident_zero, 1)
            nc.gpsimd.affine_select(out=ident[:, :], in_=ident[:, :], compare_op=ALU.not_equal, fill=1.0,
                                    base=0, pattern=[[-1, P]], channel_multiplier=1).then_inc(ident_set, 1)
            pool.wait_ge(ones_set, 2)

            def epilogue(layer, q):
                Q = NQ * layer + q
                step = [0]

                def link(ins):
                    step[0] += 1
                    ins.then_inc(pdone[layer], 1)
                    pool.wait_ge(pdone[layer], EPI[layer] * q + step[0])
                    apart(pool, EPI[layer] * q + step[0])

                numf, tmpf = num[:, :, 0:F], tmp[:, :, 0:F]
                pool.wait_ge(acc_free, TI * (Q + 1))
                apart(pool, TI * (Q + 1))
                pool.wait_ge(exps, 4 * (layer + 1))
                link(nc.gpsimd.tensor_tensor(num, part[:, :, 0, :], wide(acol[:, 0, q, :], FD), ALU.mult))
                link(nc.gpsimd.tensor_tensor(tmp, part[:, :, 1, :], wide(acol[:, 1, q, :], FD), ALU.mult))
                link(nc.gpsimd.tensor_tensor(num, num, tmp, ALU.add))
                link(nc.gpsimd.tensor_scalar(zero_row, num[:, :, F], 0.0, None, ALU.is_equal))
                link(nc.gpsimd.tensor_tensor(den, num[:, :, F], zero_row, ALU.add))
                pool.wait_ge(mean_set, layer + 1)
                link(nc.gpsimd.tensor_tensor(tmpf, wide(zero_row, F),
                                             meanv[:, :].unsqueeze(1).broadcast_to([P, TI, F]), ALU.mult))
                link(nc.gpsimd.tensor_tensor(numf, numf, tmpf, ALU.add))
                pool.wait_ge(recips, Q + 1)
                apart(pool, Q + 1)
                link(nc.gpsimd.tensor_tensor(numf, numf, wide(rden, F), ALU.mult))
                if layer == 1:
                    link(nc.gpsimd.tensor_scalar(tmpf, numf, 0.0, None, ALU.min))
                    link(nc.gpsimd.tensor_scalar(numf, numf, 0.0, None, ALU.max))
                    pool.wait_ge(elu_exp, q + 1)
                    apart(pool, q + 1)
                    link(nc.gpsimd.tensor_scalar(tmpf, tmpf, -1.0, None, ALU.add))
                    link(nc.gpsimd.tensor_tensor(numf, numf, tmpf, ALU.add))
                pool.wait_ge(res_landed, 16 * (Q + 1))
                apart(pool, 16 * (Q + 1))
                link(nc.gpsimd.tensor_tensor(numf, numf, resid[:, :, :], ALU.add))
                pool.wait_ge(bn_done, TI * (Q + 1))
                apart(pool, TI * (Q + 1))
                link(nc.gpsimd.tensor_scalar(var, mv[:, :, 1], EPS, None, ALU.add))
                link(nc.gpsimd.tensor_tensor(rstd, var, mhalf, ALU.pow))
                link(nc.gpsimd.tensor_tensor(numf, numf, wide(mv[:, :, 0], F), ALU.subtract))
                if later(16 * Q):
                    pool.wait_ge(stored, 16 * Q)
                    apart(pool, 16 * Q)
                if layer == 0:
                    if later(NQ + q):
                        pool.wait_ge(grp_turned, NQ + q)
                        apart(pool, NQ + q)
                link(nc.gpsimd.tensor_tensor(xout[:, :, :], numf, wide(rstd, F), ALU.mult))
                assert step[0] == EPI[layer]

            with pool.Fori(0, NQ) as q:
                epilogue(0, q)
            with pool.Fori(0, NQ) as q:
                epilogue(1, q)

        def w_piece(layer, g):
            cs = slice(8 * g, 8 * g + 8)
            for side in range(2):
                t = scr[:, side, :].rearrange("p (c f) -> p c f", f=FD)
                yield side, t, [wmov[:, cs, side, i, :] for i in range(SPLIT)], cs

        @block.scalar
        def _(act):
            def copy_xt(n, bank):
                act.wait_ge(grp_turned, n + 1)
                if later(n):
                    act.wait_ge(grp_row, n)
                nc.scalar.copy(xt, bank[0:F, :]).then_inc(xt_set, 1)

            act.wait_ge(wt_turned, 1)
            nc.scalar.copy(wl1[:, F:2 * F], srcb[0:F, 0:F]).then_inc(wt_copied, 1)
            for g in range(NQ):
                copy_xt(g, acc[g % 2])

            def begin(layer):
                act.wait_ge(centred, 3 * (layer + 1))
                a = SLOPE[layer]
                nc.scalar.activation(bcol[:, 0, :], dcen[:, :], ACT.Exp).then_inc(exps, 1)
                nc.scalar.activation(bcol[:, 1, :], dcen[:, :], ACT.Exp, scale=a).then_inc(exps, 1)
                flat = acol[:, :, :, :].rearrange("p s q t -> p s (q t)")
                nc.scalar.activation(flat[:, 0, :], scen[:, 0, :], ACT.Exp, scale=1 - a).then_inc(exps, 1)
                nc.scalar.activation(flat[:, 1, :], scen[:, 1, :], ACT.Exp, scale=a - 1).then_inc(exps, 1)

            def body(layer, q, prep, epi):
                Q = NQ * layer + q
                for k in range(KB):
                    u = KB * Q + k
                    if isinstance(q, int) and q == 0 and k < 4:
                        for lot in range(2):
                            for side, t, parts, _ in w_piece(layer, k):
                                act.wait_ge(w_vec, 24 * layer + 6 * k + 2 * lot + side + 1)
                                nc.scalar.copy(parts[lot], t).then_inc(w_act, 1)
                    if k == 0:
                        act.wait_ge(srcb_set, Q + 1)
                    if later(u - SR + 1):
                        act.wait_ge(mm_done, u - SR + 1)
                    for b in range(NB):
                        c = NB * k + b
                        ins = nc.scalar.activation(neg[:, k % SR, :, b], srcb[:, :], ACT.Sign,
                                                   bias=dcol[:, layer, c:c + 1])
                    ins.then_inc(signs, 1)
                    if layer == 1 and epi and k == 5:
                        elu(q - 1)
                if epi and layer == 0:
                    copy_xt(NQ + q - 1, pg)

            def elu(q):
                act.wait_ge(pdone[1], EPI[1] * q + 9)
                nc.scalar.activation(tmp[:, :, 0:F], tmp[:, :, 0:F], ACT.Exp).then_inc(elu_exp, 1)

            def between():
                copy_xt(2 * NQ - 1, pg)
                begin(1)

            begin(0)
            all_supertiles(act, body, between)
            elu(NQ - 1)

        @block.vector
        def _(dve):
            dve.wait_ge(ident_set, 1)
            nc.vector.memset(val[:, :, F], 1.0).then_inc(consts, 1)
            nc.vector.memset(s8, 0.0).then_inc(consts, 1)
            nc.vector.memset(selall[:, :, :], 0.0).then_inc(consts, 1)
            nc.vector.tensor_scalar(notid[F:F + NQ, :], ident[F:F + NQ, F:F + NQ], -1.0, 1.0, ALU.mult, ALU.add)\
                .then_inc(consts, 1)
            nc.vector.tensor_copy(proj[:, 0, 0:F], ident[0:F, 0:F]).then_inc(consts, 1)
            dve.wait_ge(w_landed, 80)
            nc.vector.tensor_copy(proj[:, 0, F:F + 1], att[:, 0, 1:2]).then_inc(consts, 1)
            nc.vector.tensor_copy(proj[:, 0, F + 1:F + 2], att[:, 0, 0:1]).then_inc(consts, 1)
            nc.vector.tensor_copy(proj[:, 1, 0:F], wl1[:, 0:F]).then_inc(consts, 1)
            dve.wait_ge(consts, 8)
            nc.vector.tensor_copy(selall[:, 0, 0:NQ * NQ:NQ + 1], att[:, 0, 0:1].broadcast_to([F, NQ]))\
                .then_inc(consts, 1)

            def second_weights():
                dve.wait_ge(wa_ready, 1)
                nc.vector.tensor_copy(proj[:, 1, F:F + 1], srcb[0:F, F + 1:F + 2]).then_inc(consts, 1)
                nc.vector.tensor_copy(proj[:, 1, F + 1:F + 2], srcb[0:F, F:F + 1]).then_inc(consts, 1)
                nc.vector.tensor_copy(selall[:, 1, 0:NQ * NQ:NQ + 1], srcb[0:F, F:F + 1].broadcast_to([F, NQ]))\
                    .then_inc(consts, 1)

            def encode(q, k):
                n = KB * q + k
                dve.wait_ge(adj_landed[k % 2], 16 * (4 * q + k // 2 + 1))
                apart(dve, 16 * (4 * q + k // 2 + 1))
                if later(n - 1):
                    dve.wait_ge(turned, n - 1)
                    apart(dve, n - 1)
                nc.vector.tensor_scalar(enc8[:, k % 2, :], adj_in[:, k % 2, :], 1.0, 0.5, ALU.min, ALU.max,
                                        saturate=False)\
                    .then_inc(encoded, 1)

            def extract(q, k):
                n = KB * q + k
                dve.wait_ge(turned, n + 1)
                apart(dve, n + 1)
                half = 4 * (k % 2)
                nc.vector.tensor_scalar(mask_t[:, q, half:half + 4, k // 2, :], tb[k % 2][:, :, :].bitcast(U32),
                                        0x08080808, 3, ALU.bitwise_and, ALU.logical_shift_left).then_inc(masked, 1)

            def group_values(n, bank):
                g = n if isinstance(n, int) and n < NQ else n - NQ
                dve.wait_ge(grp_proj, n + 1)
                apart(dve, n + 1)
                v = bank[:, 0:NB * FD].rearrange("p (b c) -> p b c", c=FD)
                vv = val[:, :, :].rearrange("p (g b) c -> p g b c", b=NB)
                dd = dcol[:, 0 if isinstance(n, int) and n < NQ else 1, :].rearrange("p (g b) -> p g b", b=NB)
                ss = scol[:, :].rearrange("p (g t) -> p g t", t=TI)
                nc.vector.tensor_copy(vv[:, g, :, 0:F], v[:, :, 0:F]).then_inc(grp_val, 1)
                nc.vector.tensor_copy(dd[:, g, :], v[:, :, F]).then_inc(grp_val, 1)
                nc.vector.tensor_copy(ss[:, g, :], bank[:, NB * FD:NB * FD + TI]).then_inc(grp_val, 1)

            def group_row(n):
                g = n if isinstance(n, int) and n < NQ else n - NQ
                dve.wait_ge(grp_row, n + 1)
                apart(dve, n + 1)
                if later(n):
                    dve.wait_ge(s8_set, n)
                    apart(dve, n)
                nc.vector.scalar_tensor_tensor(out=s8, in0=s8, scalar=notid[F:F + NQ, bass.ds(g, 1)],
                                               in1=pg[F:F + NQ, :], op0=ALU.mult, op1=ALU.add).then_inc(s8_set, 1)

            def set_pick(Q, q):
                if later(Q):
                    dve.wait_ge(srcb_set, Q)
                    apart(dve, Q)
                nc.vector.tensor_copy(pick[F:F + NQ, :], ident[F:F + NQ, bass.ds(F + q, 1)].broadcast_to([NQ, P]))\
                    .then_inc(picked, 1)

            def set_sel(n, g):
                if later(n):
                    dve.wait_ge(grp_row, n)
                    apart(dve, n)
                nc.vector.tensor_copy(selq[:, :], selall[:, 1, :].rearrange("f (a b) -> f a b", b=NQ)[:, g, :])\
                    .then_inc(sel_set, 1)

            for g in range(NQ):
                encode(0, g)
                if g == 0:
                    second_weights()
                group_values(g, acc[2 + g % 2])
                group_row(g)
                extract(0, g)

            def begin(layer):
                dve.wait_ge(grp_val, 3 * NQ * (layer + 1))
                nc.vector.tensor_reduce(stat[:, 0:1], dcol[:, layer, :], AX.X, ALU.max).then_inc(stat_set, 1)
                nc.vector.tensor_reduce(stat[:, 1:2], dcol[:, layer, :], AX.X, ALU.min, negate=True).then_inc(stat_set, 1)
                set_pick(NQ * layer, 0)
                dve.wait_ge(stat_turned, layer + 1)
                nc.vector.tensor_reduce(gst[:, 0:1], pg[0:2, 0:P], AX.X, ALU.max).then_inc(gst_set, 1)
                dve.wait_ge(gst_set, 2 * layer + 1)
                nc.vector.tensor_scalar(gst[:, 2:4], ident[0:2, 0:2], gst[:, 0:1], None, ALU.mult)\
                    .then_inc(gst_set, 1)
                dve.wait_ge(max_spread, layer + 1)
                nc.vector.tensor_copy(cmax[:, :], pg[:, P:P + 2]).then_inc(cmax_set, 1)
                dve.wait_ge(cmax_set, layer + 1)
                nc.vector.tensor_scalar(dcen[:, :], dcol[:, layer, :], cmax[:, 0:1], None, ALU.subtract)\
                    .then_inc(centred, 1)
                nc.vector.tensor_scalar(scen[:, 0, :], scol[:, :], cmax[:, 0:1], 0.0, ALU.add, ALU.min)\
                    .then_inc(centred, 1)
                nc.vector.tensor_scalar(scen[:, 1, :], scol[:, :], cmax[:, 0:1], 0.0, ALU.add, ALU.max)\
                    .then_inc(centred, 1)
                dve.wait_ge(exps, 4 * layer + 2)

            def weigh(layer, g):
                base_v, base_a = 24 * layer + 6 * g, 16 * layer + 4 * g
                for side, t, parts, cs in w_piece(layer, g):
                    if later(base_v):
                        dve.wait_ge(w_vec, base_v)
                    nc.vector.tensor_tensor(t, val[:, cs, :], bcol[:, side, cs].unsqueeze(2)
                                            .broadcast_to([P, 8, FD]), ALU.mult).then_inc(w_vec, 1)
                for side, t, parts, cs in w_piece(layer, g):
                    dve.wait_ge(w_act, base_a + side + 1)
                    nc.vector.tensor_tensor(t, t, parts[0], ALU.subtract).then_inc(w_vec, 1)
                for side, t, parts, cs in w_piece(layer, g):
                    dve.wait_ge(w_act, base_a + 2 + side + 1)
                    nc.vector.tensor_tensor(parts[2], t, parts[1], ALU.subtract).then_inc(w_vec, 1)

            def masks(layer, q, k):
                Q = NQ * layer + q
                u = KB * Q + k
                bits = mask_t[:, q, k, :, :].rearrange("p t i -> p (t i)").bitcast(U16)
                dve.wait_ge(signs, u + 1)
                apart(dve, u + 1)
                if layer == 0 and k == 0:
                    dve.wait_ge(masked, KB * (q + 1))
                    apart(dve, KB * (q + 1))
                nc.vector.tensor_tensor(neg16[:, k % SR, :], neg16[:, k % SR, :], bits, ALU.bitwise_and)\
                    .then_inc(negs, 1)
                if later(u - MR + 1):
                    dve.wait_ge(mm_done, u - MR + 1)
                    apart(dve, u - MR + 1)
                dve.wait_ge(negs, u + 1)
                apart(dve, u + 1)
                nc.vector.tensor_tensor(pos16[:, k % MR, :], neg16[:, k % SR, :], bits, ALU.bitwise_xor)\
                    .then_inc(poss, 1)

            def sum_parts(layer, q):
                Q = NQ * layer + q
                if layer == 0:
                    if later(EPI[0] * q):
                        dve.wait_ge(pdone[0], EPI[0] * q)
                        apart(dve, EPI[0] * q)
                elif isinstance(q, int) and q == 0:
                    dve.wait_ge(pdone[0], EPI[0] * NQ)
                else:
                    dve.wait_ge(pdone[1], EPI[1] * q)
                    apart(dve, EPI[1] * q)
                for t in range(TI):
                    if t < TI - 1:
                        dve.wait_ge(acc_ready, (TI - 1) * Q + t + 1)
                        apart(dve, (TI - 1) * Q + t + 1)
                    else:
                        dve.wait_ge(mm_done, KB * (Q + 1))
                        apart(dve, KB * (Q + 1))
                    nc.vector.tensor_reduce(
                        part[:, t, :, :],
                        acc[t][:, 0:2 * WC].rearrange("p (s r c) -> p s c r", s=2, r=SPLIT),
                        AX.X, ALU.add).then_inc(acc_free, 1)

            def take_reciprocal(layer, q):
                dve.wait_ge(pdone[layer], EPI[layer] * q + 5)
                apart(dve, EPI[layer] * q + 5)
                nc.vector.reciprocal(rden, den).then_inc(recips, 1)

            def take_stats(layer, q):
                Q = NQ * layer + q
                dve.wait_ge(pdone[layer], EPI[layer] * (q + 1) - 4)
                apart(dve, EPI[layer] * (q + 1) - 4)
                for t in range(TI):
                    nc.vector.bn_stats(bst[:, t, :], num[:, t, 0:F]).then_inc(bn_part, 1)
                dve.wait_ge(bn_part, TI * (Q + 1))
                apart(dve, TI * (Q + 1))
                for t in range(TI):
                    nc.vector.bn_aggr(mv[:, t, :], bst[:, t, :]).then_inc(bn_done, 1)

            def body(layer, q, prep, epi):
                Q = NQ * layer + q
                for k in range(KB):
                    if isinstance(q, int) and q == 0 and k < 4:
                        weigh(layer, k)
                    if prep and k == 0:
                        encode(q + 1, 0)
                    masks(layer, q, k)
                    if prep:
                        if k < KB - 1:
                            encode(q + 1, k + 1)
                        extract(q + 1, k)
                    if isinstance(q, int) and q == 0 and k == 3:
                        mean_rows(layer)
                    if isinstance(q, int) and q == 0 and k == 6:
                        mean(layer)
                    if epi:
                        if k == 0:
                            sum_parts(layer, q - 1)
                        if k == 2:
                            take_reciprocal(layer, q - 1)
                        if k == (4 if layer == 0 else 7):
                            take_stats(layer, q - 1)
                        if layer == 0 and k == 5:
                            set_sel(NQ + q - 1, q - 1)
                        if layer == 0 and k == 6:
                            group_values(NQ + q - 1, pg)
                    if k == 6 and not (isinstance(q, int) and q == NQ - 1):
                        set_pick(Q + 1, q + 1)
                    if epi and layer == 0 and k == 7:
                        group_row(NQ + q - 1)

            def mean_rows(layer):
                nc.vector.tensor_reduce(meanv[:, :], val[:, :, 0:F].rearrange("p c f -> p f c"), AX.X, ALU.add)\
                    .then_inc(mean_sum, 1)

            def mean(layer):
                dve.wait_ge(mean_ps, layer + 1)
                nc.vector.tensor_scalar(meanv[:, :], pg[:, 0:F], 1.0 / N, None, ALU.mult).then_inc(mean_set, 1)

            def finish(layer):
                sum_parts(layer, NQ - 1)
                take_reciprocal(layer, NQ - 1)
                take_stats(layer, NQ - 1)

            def between():
                finish(0)
                set_sel(2 * NQ - 1, NQ - 1)
                group_values(2 * NQ - 1, pg)
                group_row(2 * NQ - 1)
                begin(1)

            begin(0)
            all_supertiles(dve, body, between)
            finish(1)

        @block.tensor
        def _(pe):
            pe.wait_ge(ident_set, 1)
            pe.wait_ge(w_landed, 80)
            nc.tensor.transpose(srcb[0:F, 0:F], wl1[:, 0:F], ident[0:F, 0:F]).then_inc(wt_turned, 1)
            pe.wait_ge(wt_copied, 1)
            nc.tensor.matmul(srcb[0:F, F:F + 2], wl1[:, F:2 * F], att[:, 1, :], start=True, stop=True)\
                .then_inc(wa_ready, 1)
            pe.wait_ge(x_landed, 16)
            pe.wait_ge(consts, 9)

            def turn_group(n, rows, bank):
                for t in range(TI):
                    ins = nc.tensor.transpose(bank[0:F, t * P:(t + 1) * P], rows[:, t, :], ident[:, :])
                ins.then_inc(grp_turned, 1)

            def project_group(n, layer, bank):
                pe.wait_ge(xt_set, n + 1)
                apart(pe, n + 1)
                for b in range(NB):
                    nc.tensor.matmul(bank[:, b * FD:(b + 1) * FD], xt[:, b:ROWS:NB], proj[:, layer, 0:FD],
                                     start=True, stop=True)
                for t in range(TI):
                    c = NB * FD + t
                    ins = nc.tensor.matmul(bank[:, c:c + 1], xt[:, t * P:(t + 1) * P], proj[:, layer, FD:FD + 1],
                                           start=True, stop=True)
                ins.then_inc(grp_proj, 1)

            def row_group(n, sel):
                nc.tensor.matmul(pg[F:F + NQ, :], sel, xt, start=True, stop=True).then_inc(grp_row, 1)

            def turn_masks(q, k):
                n = KB * q + k
                pe.wait_ge(encoded, n + 1)
                apart(pe, n + 1)
                if later(n - 1):
                    pe.wait_ge(masked, n - 1)
                    apart(pe, n - 1)
                for j in range(4):
                    ins = nc.tensor.transpose(tb[k % 2][:, j, :], enc[:, k % 2, j * P:(j + 1) * P], ident[:, :])
                ins.then_inc(turned, 1)

            for g in range(NQ + 1):
                if g < NQ:
                    if later(g - 1):
                        pe.wait_ge(xt_set, g - 1)
                    turn_group(g, x_all[:, TI * g:TI * g + TI, :], acc[g % 2])
                if g > 0:
                    n = g - 1
                    if later(3 * (n - 1)):
                        pe.wait_ge(grp_val, 3 * (n - 1))
                        apart(pe, 3 * (n - 1))
                    project_group(n, 0, acc[2 + n % 2])
                    if later(n):
                        pe.wait_ge(s8_set, n)
                        apart(pe, n)
                    row_group(n, selall[:, 0, :].rearrange("f (a b) -> f a b", b=NQ)[:, n, :])
                    turn_masks(0, n)

            def spread_rows(Q):
                pe.wait_ge(picked, Q + 1)
                apart(pe, Q + 1)
                if later(KB * Q):
                    pe.wait_ge(signs, KB * Q)
                    apart(pe, KB * Q)
                nc.tensor.matmul(srcb[:, :], pick[F:F + NQ, :], s8, start=True, stop=True).then_inc(srcb_set, 1)

            def begin(layer):
                pe.wait_ge(stat_set, 2 * (layer + 1))
                pe.wait_ge(s8_set, NQ * (layer + 1))
                nc.tensor.transpose(pg[0:2, 0:P], stat[:, :], ident[:, :]).then_inc(stat_turned, 1)
                spread_rows(NQ * layer)
                pe.wait_ge(gst_set, 2 * (layer + 1))
                nc.tensor.matmul(pg[:, P:P + 2], ones[0:2, :], gst[:, 2:4], start=True, stop=True)\
                    .then_inc(max_spread, 1)

            def products(layer, q, k):
                Q = NQ * layer + q
                u = KB * Q + k
                pe.wait_ge(negs, u + 1)
                apart(pe, u + 1)
                pe.wait_ge(poss, u + 1)
                apart(pe, u + 1)
                if isinstance(q, int) and q == 0:
                    pe.wait_ge(w_vec, 24 * layer + 6 * min(k // 2 + 1, 4))
                for t in range(TI):
                    if k == 0:
                        if later(TI * (Q - 1) + t + 1):
                            pe.wait_ge(acc_free, TI * (Q - 1) + t + 1)
                            apart(pe, TI * (Q - 1) + t + 1)
                    for b in range(NB):
                        for side, m in enumerate((pos8[:, k % MR], neg8[:, k % SR])):
                            first = k == 0 and b == 0 and side == 0
                            last = k == KB - 1 and b == NB - 1 and side == 1
                            ins = nc.tensor.matmul(
                                acc[t][:, side * WC:(side + 1) * WC], m[:, t * P:(t + 1) * P, b],
                                wmov[:, NB * k + b, side, :, :].rearrange("p r c -> p (r c)"),
                                start=first, stop=last, skip_group_check=True)
                    if k == KB - 1 and t < TI - 1:
                        ins.then_inc(acc_ready, 1)
                ins.then_inc(mm_done, 1)

            def body(layer, q, prep, epi):
                Q = NQ * layer + q
                for k in range(KB):
                    if prep:
                        turn_masks(q + 1, k)
                    if epi and layer == 0:
                        n = NQ + q - 1
                        if k == 5:
                            pe.wait_ge(pdone[0], EPI[0] * q)
                            apart(pe, EPI[0] * q)
                            pe.wait_ge(mean_set, 1)
                            if later(n):
                                pe.wait_ge(s8_set, n)
                                apart(pe, n)
                            turn_group(n, xout, pg)
                        if k == 6:
                            project_group(n, 1, pg)
                        if k == 7:
                            pe.wait_ge(grp_val, 3 * (n + 1))
                            apart(pe, 3 * (n + 1))
                            pe.wait_ge(sel_set, q)
                            apart(pe, q)
                            if not (isinstance(q, int) and q == NQ - 1):
                                spread_rows(Q + 1)
                            row_group(n, selq[:, :])
                    elif k == 7:
                        if not (isinstance(q, int) and q == NQ - 1):
                            spread_rows(Q + 1)
                    if isinstance(q, int) and q == 0 and k == 5:
                        mean(layer)
                    products(layer, q, k)

            def mean(layer):
                pe.wait_ge(mean_sum, layer + 1)
                pe.wait_ge(cmax_set, layer + 1)
                nc.tensor.matmul(pg[:, 0:F], ones[:, :], meanv[:, :], start=True, stop=True).then_inc(mean_ps, 1)

            def between():
                n = 2 * NQ - 1
                pe.wait_ge(pdone[0], EPI[0] * NQ)
                if later(n):
                    pe.wait_ge(s8_set, n)
                    apart(pe, n)
                turn_group(n, xout, pg)
                project_group(n, 1, pg)
                pe.wait_ge(grp_val, 3 * (n + 1))
                apart(pe, 3 * (n + 1))
                pe.wait_ge(sel_set, NQ)
                row_group(n, selq[:, :])
                begin(1)

            pe.wait_ge(consts, 12)
            begin(0)
            all_supertiles(pe, body, between)


def program(nc, x, adj, a0, w1, a1, x1_dram, out):
    fast_attention(nc, x, adj, a0, w1, a1, x1_dram, out)


def kernel(x, adj, L0_gnn_a, L1_gnn_W, L1_gnn_a):
    import numpy as _np
    import concourse.bacc as _bacc
    from concourse import mybir as _mybir
    from concourse.bass_utils import run_bass_kernel_spmd as _run

    nc = _bacc.Bacc("TRN2", target_bir_lowering=False, num_devices=1)
    arrays, args = {}, []
    for name, a in (("x", x), ("adj", adj), ("a0", L0_gnn_a), ("w1", L1_gnn_W), ("a1", L1_gnn_a)):
        a = _np.ascontiguousarray(a)
        arrays[f"in_{name}"] = a
        args.append(nc.dram_tensor(f"in_{name}", a.shape, _mybir.dt.from_np(a.dtype), kind="ExternalInput").ap())
    args.append(nc.dram_tensor("x1_rows", (N, F), F32, kind="Internal").ap())
    args.append(nc.dram_tensor("out_0", (N, F), F32, kind="ExternalOutput").ap())
    program(nc, *args)
    r = _run(nc, [arrays], core_ids=[0])
    return r.results[0]["out_0"]
```

```python
from contextlib import ExitStack

import concourse.bass as bass
from concourse import mybir

P = 128
N = 4096
F = 64
NQ = 8
TI = 4
KB = 8
NB = 4
ROWS = TI * P
HALF = N // 2
VCOLS = 1792
FD = F + 1
SPLIT = 3
WC = SPLIT * FD
SR = 4
MR = 2
SLOPE = (0.01, 0.2)
EPS = 1e-5
NO_EDGE = 0x30
EPI = (13, 17)
EARLY = 6 * NB
WEIGH_V, WEIGH_A = 6, 4

ALU = mybir.AluOpType
ACT = mybir.ActivationFunctionType
AX = mybir.AxisListType
F32 = mybir.dt.float32
BF16 = mybir.dt.bfloat16
FP8 = mybir.dt.float8e4
I32 = mybir.dt.int32
U32 = mybir.dt.uint32
U16 = mybir.dt.uint16
U8 = mybir.dt.uint8
I8 = mybir.dt.int8


def fast_attention(nc, x, adj, a0, w1, a1, x1_dram, out):
    with ExitStack() as ctx:
        def sb(name, shape, dt):
            return ctx.enter_context(nc.sbuf_tensor(name, shape, dt))

        def ps(name, shape, dt):
            return ctx.enter_context(nc.psum_tensor(name, shape, dt))

        def sem(name):
            return ctx.enter_context(nc.semaphore(name))

        mask_t = sb("mask_t", [P, NQ, KB, TI, P], U32)
        stage = sb("stage", [P, 2 * HALF + 2 * HALF // NB], U32)
        neg = sb("neg", [P, SR, ROWS, NB], I8)
        pos = sb("pos", [P, MR, ROWS, NB], I8)
        wmov = sb("wmov", [P, KB * NB, 2 * WC], BF16)
        val = sb("val", [P, KB * NB, FD], F32)
        prod = sb("prod", [P, 2, NB, FD], F32)
        xt = sb("xt", [F, ROWS], F32)
        scr = sb("scr", [P, 2, 2 * TI * FD], F32)
        resid = sb("resid", [P, TI, F], F32)
        xout = sb("xout", [P, TI, F], F32)
        ident = sb("ident", [P, P], F32)
        ones = sb("ones", [P, P], F32)
        att0 = sb("att0", [P, 2, F], F32)
        att1 = sb("att1", [F, 2], F32)
        wl1 = sb("wl1", [F, 2 * F], F32)
        proj = sb("proj", [F, F + 2], F32)
        dcol = sb("dcol", [P, 2, KB * NB], F32)
        scol = sb("scol", [P, 2, NQ, TI], F32)
        scur = sb("scur", [P, TI], F32)
        dcen = sb("dcen", [P, KB * NB], F32)
        scen = sb("scen", [P, 2, NQ * TI], F32)
        bcol = sb("bcol", [P, 2, KB * NB], F32)
        acol = sb("acol", [P, 2, 2, NQ, TI], F32)
        stat = sb("stat", [P, 2], F32)
        gst = sb("gst", [2, 4], F32)
        cmax = sb("cmax", [P, 2, 2], F32)
        meanv = sb("meanv", [P, F], F32)
        small = sb("small", [P, 6, TI], F32)
        bst = sb("bst", [P, TI, 6], F32)
        mv = sb("mv", [P, TI, 2], F32)

        def spare(q, half):
            flat = mask_t[:, q, :, :, :].rearrange("p k t i -> p (k t i)").bitcast(F32)
            return flat[:, half * NQ * TI * F:(half + 1) * NQ * TI * F].rearrange("p (t d) -> p t d", d=F)

        x_all, s_prod, d_prod = spare(NQ - 1, 0), spare(NQ - 1, 1), spare(NQ - 2, 0)

        acc = [ps(f"acc{t}", [P, 512], F32) for t in range(TI)]
        tb = ps("tb", [P, 4, P], F32)
        pg = ps("pg", [P, 512], F32)
        srcb = ps("srcb", [P, 2, 512], F32)

        x_landed = sem("x_landed")
        val_landed = sem("val_landed")
        w_landed = sem("w_landed")
        adj_landed = [sem(f"adj_landed{i}") for i in range(2)]
        res_landed = sem("res_landed")
        stored = sem("stored")
        ones_set = sem("ones_set")
        ident_zero = sem("ident_zero")
        ident_set = sem("ident_set")
        ones_col = sem("ones_col")
        wt_turned = sem("wt_turned")
        wt_copied = sem("wt_copied")
        wa_ready = sem("wa_ready")
        proj_set = sem("proj_set")
        s_mult = sem("s_mult")
        d_mult = sem("d_mult")
        s_set = sem("s_set")
        d_set = sem("d_set")
        enc_vec = sem("enc_vec")
        enc_pool = sem("enc_pool")
        turned = sem("turned")
        masked = sem("masked")
        rows_turned = sem("rows_turned")
        xt_set = sem("xt_set")
        projected = sem("projected")
        grp_set = sem("grp_set")
        scur_set = sem("scur_set")
        spread = sem("spread")
        stat_set = sem("stat_set")
        stat_turned = sem("stat_turned")
        gst_set = sem("gst_set")
        max_spread = sem("max_spread")
        cmax_set = sem("cmax_set")
        dcen_set = sem("dcen_set")
        b_set = sem("b_set")
        scen_set = sem("scen_set")
        a_set = sem("a_set")
        w_vec = sem("w_vec")
        w_act = sem("w_act")
        mean_sum = sem("mean_sum")
        mean_ps = sem("mean_ps")
        mean_set = sem("mean_set")
        signs = sem("signs")
        negs = sem("negs")
        poss = sem("poss")
        mm_done = sem("mm_done")
        acc_ready = sem("acc_ready")
        acc_free = sem("acc_free")
        pdone = [sem(f"pdone{i}") for i in range(2)]
        recips = sem("recips")
        bn_part = sem("bn_part")
        bn_done = sem("bn_done")
        elu_exp = sem("elu_exp")

        adj_v = adj.rearrange("(q t p) (h j) -> q t h p j", t=TI, p=P, h=2)
        x_v = x.rearrange("(q t p) d -> q p t d", t=TI, p=P)
        x1_v = x1_dram.rearrange("(q t p) d -> q p t d", t=TI, p=P)
        out_v = out.rearrange("(q t p) d -> q p t d", t=TI, p=P)

        adj_in = stage[:, 0:2 * HALF].bitcast(I32).rearrange("p (s j) -> p s j", s=2)
        enc = stage[:, 2 * HALF:].bitcast(F32).rearrange("p (s w) -> p s w", s=2)
        enc8 = stage[:, 2 * HALF:].bitcast(U8).rearrange("p (s w) -> p s w", s=2)
        w_early = stage[:, 0:EARLY * WC].bitcast(BF16).rearrange("p (c w) -> p c w", w=2 * WC)
        neg16 = neg[:, :, :, :].rearrange("p r i b -> p r (i b)").bitcast(U16)
        pos16 = pos[:, :, :, :].rearrange("p r i b -> p r (i b)").bitcast(U16)
        neg8 = neg[:, :, :, :].bitcast(FP8)
        pos8 = pos[:, :, :, :].bitcast(FP8)
        part = scr[:, 0, :].rearrange("p (t s c) -> p t s c", t=TI, s=2)
        num = scr[:, 1, 0:TI * FD].rearrange("p (t c) -> p t c", t=TI)
        tmp = scr[:, 1, TI * FD:2 * TI * FD].rearrange("p (t c) -> p t c", t=TI)
        zero_row, den, rden, var, rstd, mhalf = (small[:, i, :] for i in range(6))

        def weighed(layer, c0, c1):
            return (w_early if layer == 1 and c1 <= EARLY else wmov)[:, c0:c1]

        def wide(col, c):
            return col.unsqueeze(2).broadcast_to([P, TI, c])

        def later(count):
            return not isinstance(count, int) or count > 0

        def apart(eng, count):
            if not isinstance(count, int):
                eng.nop(nofuse=True)

        def is_first(q):
            return isinstance(q, int) and q == 0

        def is_last(q):
            return isinstance(q, int) and q == NQ - 1

        def all_supertiles(eng, body):
            for layer in range(2):
                body(layer, 0)
                with eng.Fori(1, NQ - 1) as q:
                    body(layer, q)
                body(layer, NQ - 1)

        def prepares(layer, q):
            return layer == 0 and not is_last(q)

        def before(layer, q):
            if is_first(q):
                return None if layer == 0 else (0, NQ - 1, NQ - 1)
            return layer, q - 1, NQ * layer + q - 1

        block = ctx.enter_context(nc.Block())

        @block.sync
        def _(sp):
            sp.dma_start(x_all, x.rearrange("(t p) d -> p t d", p=P)).then_inc(x_landed, 16)
            sp.dma_start(att0[:, :, :], a0.rearrange("(s d) o -> o s d", s=2).partition_broadcast(P)
                         .rearrange("p o s d -> p (o s) d")).then_inc(w_landed, 16)

            def load_adj(q, k):
                if later(KB * q + k - 1):
                    sp.wait_ge(enc_vec, KB * q + k - 1)
                    sp.wait_ge(enc_pool, KB * q + k - 1)
                sp.dma_start(adj_in[:, k % 2, :], adj_v[q, k // 2, k % 2]).then_inc(adj_landed[k % 2], 16)

            load_adj(0, 0)
            for k in range(KB):
                sp.dma_start(val[:, NB * k:NB * (k + 1), 0:F], x.rearrange("(k p b) d -> k p b d", p=P, b=NB)[k])\
                    .then_inc(val_landed, 16)
            for half in range(2):
                sp.dma_start(att1[:, half:half + 1], a1[half * F:(half + 1) * F, :]).then_inc(w_landed, 16)
            sp.dma_start(wl1[:, 0:F], w1).then_inc(w_landed, 16)
            for k in range(1, KB):
                load_adj(0, k)

            def store(layer, q):
                sp.wait_ge(pdone[layer], EPI[layer] * (q + 1))
                sp.dma_start((x1_v if layer == 0 else out_v)[q], xout[:, :, :]).then_inc(stored, 16)

            def load_resid(layer, q):
                if layer == 1:
                    sp.wait_ge(stored, 16 * NQ)
                sp.dma_start(resid[:, :, :], (x_v if layer == 0 else x1_v)[q]).then_inc(res_landed, 16)

            def body(layer, q):
                if prepares(layer, q):
                    for k in range(KB):
                        load_adj(q + 1, k)
                if before(layer, q) is not None:
                    store(*before(layer, q)[0:2])
                load_resid(layer, q)

            all_supertiles(sp, body)
            store(1, NQ - 1)
            sp.wait_ge(stored, 16 * 2 * NQ)

        @block.gpsimd
        def _(pool):
            nc.gpsimd.memset(ident[:, :], 0.0).then_inc(ident_zero, 1)
            nc.gpsimd.memset(ones[:, :], 1.0).then_inc(ones_set, 1)
            nc.gpsimd.memset(mhalf, -0.5).then_inc(ones_set, 1)
            pool.wait_ge(ident_zero, 1)
            nc.gpsimd.affine_select(out=ident[:, :], in_=ident[:, :], compare_op=ALU.not_equal, fill=1.0,
                                    base=0, pattern=[[-1, P]], channel_multiplier=1).then_inc(ident_set, 1)
            nc.gpsimd.memset(val[:, :, F:FD], 1.0).then_inc(ones_col, 1)
            pool.wait_ge(ones_set, 2)

            def encode(q, k):
                pool.wait_ge(adj_landed[k % 2], 16 * (4 * q + k // 2 + 1))
                if later(KB * q + k - 1):
                    pool.wait_ge(turned, KB * q + k - 1)
                apart(pool, q)
                nc.gpsimd.tensor_scalar(enc8[:, k % 2, VCOLS:HALF], adj_in[:, k % 2, VCOLS:HALF], 0.0, float(NO_EDGE),
                                        ALU.is_gt, ALU.add).then_inc(enc_pool, 1)

            def epilogue_sums(layer, q, Q):
                done, base = pdone[layer], EPI[layer] * q
                numf, tmpf = num[:, :, 0:F], tmp[:, :, 0:F]
                pool.wait_ge(acc_free, TI * (Q + 1))
                pool.wait_ge(a_set, 2 * (layer + 1))
                nc.gpsimd.tensor_tensor(num, part[:, :, 0, :], wide(acol[:, layer, 0, q, :], FD), ALU.mult)\
                    .then_inc(done, 1)
                nc.gpsimd.tensor_tensor(tmp, part[:, :, 1, :], wide(acol[:, layer, 1, q, :], FD), ALU.mult)\
                    .then_inc(done, 1)
                pool.wait_ge(done, base + 2)
                nc.gpsimd.tensor_tensor(num, num, tmp, ALU.add).then_inc(done, 1)

            def epilogue_empty_rows(layer, q, Q):
                done, base = pdone[layer], EPI[layer] * q
                numf, tmpf = num[:, :, 0:F], tmp[:, :, 0:F]
                pool.wait_ge(done, base + 3)
                apart(pool, q)
                nc.gpsimd.tensor_scalar(zero_row, num[:, :, F], 0.0, None, ALU.is_equal).then_inc(done, 1)
                pool.wait_ge(done, base + 4)
                nc.gpsimd.tensor_tensor(den, num[:, :, F], zero_row, ALU.add).then_inc(done, 1)
                pool.wait_ge(mean_set, layer + 1)
                nc.gpsimd.tensor_tensor(tmpf, wide(zero_row, F), meanv[:, :].unsqueeze(1)
                                        .broadcast_to([P, TI, F]), ALU.mult).then_inc(done, 1)
                pool.wait_ge(done, base + 6)
                nc.gpsimd.tensor_tensor(numf, numf, tmpf, ALU.add).then_inc(done, 1)

            def epilogue_divide(layer, q, Q):
                done, base = pdone[layer], EPI[layer] * q
                numf, tmpf = num[:, :, 0:F], tmp[:, :, 0:F]
                pool.wait_ge(recips, Q + 1)
                pool.wait_ge(done, base + 7)
                nc.gpsimd.tensor_tensor(numf, numf, wide(rden, F), ALU.mult).then_inc(done, 1)
                pool.wait_ge(done, base + 8)
                if layer == 1:
                    apart(pool, q)
                    nc.gpsimd.tensor_scalar(tmpf, numf, 0.0, None, ALU.min).then_inc(done, 1)
                    pool.wait_ge(done, base + 9)
                    apart(pool, q)
                    nc.gpsimd.tensor_scalar(numf, numf, 0.0, None, ALU.max).then_inc(done, 1)
                    pool.wait_ge(elu_exp, q + 1)
                    apart(pool, q)
                    nc.gpsimd.tensor_scalar(tmpf, tmpf, -1.0, None, ALU.add).then_inc(done, 1)
                    pool.wait_ge(done, base + 11)
                    nc.gpsimd.tensor_tensor(numf, numf, tmpf, ALU.add).then_inc(done, 1)
                    pool.wait_ge(done, base + 12)
                pool.wait_ge(res_landed, 16 * (Q + 1))
                nc.gpsimd.tensor_tensor(numf, numf, resid[:, :, :], ALU.add).then_inc(done, 1)

            def epilogue_norm(layer, q, Q):
                done, end = pdone[layer], EPI[layer] * (q + 1)
                numf = num[:, :, 0:F]
                pool.wait_ge(bn_done, TI * (Q + 1))
                apart(pool, q)
                nc.gpsimd.tensor_scalar(var, mv[:, :, 1], EPS, None, ALU.add).then_inc(done, 1)
                pool.wait_ge(done, end - 3)
                nc.gpsimd.tensor_tensor(rstd, var, mhalf, ALU.pow).then_inc(done, 1)
                nc.gpsimd.tensor_tensor(numf, numf, wide(mv[:, :, 0], F), ALU.subtract).then_inc(done, 1)
                pool.wait_ge(done, end - 1)
                if later(Q):
                    pool.wait_ge(stored, 16 * Q)
                if layer == 1:
                    pool.wait_ge(rows_turned, NQ)
                elif later(q):
                    pool.wait_ge(rows_turned, q)
                nc.gpsimd.tensor_tensor(xout[:, :, :], numf, wide(rstd, F), ALU.mult).then_inc(done, 1)

            for k in range(KB):
                encode(0, k)

            def body(layer, q):
                prep, done = prepares(layer, q), before(layer, q)
                stages = {2: epilogue_sums, 3: epilogue_empty_rows, 4: epilogue_divide, 6: epilogue_norm}
                for k in range(KB):
                    if prep:
                        encode(q + 1, k)
                    if done is not None and k in stages:
                        stages[k](*done)

            all_supertiles(pool, body)
            epilogue_sums(1, NQ - 1, 2 * NQ - 1)
            epilogue_empty_rows(1, NQ - 1, 2 * NQ - 1)
            epilogue_divide(1, NQ - 1, 2 * NQ - 1)
            epilogue_norm(1, NQ - 1, 2 * NQ - 1)

        @block.scalar
        def _(act):
            act.wait_ge(wt_turned, 1)
            nc.scalar.copy(wl1[:, F:2 * F], pg[0:F, 0:F]).then_inc(wt_copied, 1)

            def exps_of_d(layer, c0, c1, n):
                act.wait_ge(dcen_set, n + 1)
                nc.scalar.activation(bcol[:, 0, c0:c1], dcen[:, c0:c1], ACT.Exp).then_inc(b_set, 1)
                nc.scalar.activation(bcol[:, 1, c0:c1], dcen[:, c0:c1], ACT.Exp, scale=SLOPE[layer])\
                    .then_inc(b_set, 1)

            def exps_of_s(layer):
                act.wait_ge(scen_set, 2 * (layer + 1))
                for side, scale in ((0, 1 - SLOPE[layer]), (1, SLOPE[layer] - 1)):
                    nc.scalar.activation(acol[:, layer, side, :, :].rearrange("p q t -> p (q t)"),
                                         scen[:, side, :], ACT.Exp, scale=scale).then_inc(a_set, 1)

            def round_parts(layer, g):
                w = weighed(layer, NB * g, NB * g + NB)
                for lot in range(2):
                    for side in range(2):
                        c = side * WC + lot * FD
                        act.wait_ge(w_vec, WEIGH_V * (NQ * layer + g) + 2 * lot + side + 1)
                        nc.scalar.copy(w[:, :, c:c + FD], prod[:, side, :, :]).then_inc(w_act, 1)

            def copy_turned(g):
                act.wait_ge(rows_turned, g + 1)
                if later(g):
                    act.wait_ge(projected, g)
                nc.scalar.copy(xt[:, :], pg[0:F, :]).then_inc(xt_set, 1)

            def elu(q):
                act.wait_ge(pdone[1], EPI[1] * q + 9)
                nc.scalar.activation(tmp[:, :, 0:F], tmp[:, :, 0:F], ACT.Exp).then_inc(elu_exp, 1)

            def body(layer, q):
                Q = NQ * layer + q
                done = before(layer, q)
                for k in range(KB):
                    if layer == 0 and is_first(q):
                        round_parts(0, k)
                    u = KB * Q + k
                    if k == 0:
                        act.wait_ge(spread, Q + 1)
                    if later(u - SR + 1):
                        act.wait_ge(mm_done, u - SR + 1)
                    apart(act, q)
                    for b in range(NB):
                        c = NB * k + b
                        if layer == 1 and is_first(q) and k == KB - 1 and b == 0:
                            copy_turned(NQ - 1)
                            exps_of_d(1, EARLY + NB, EARLY + 2 * NB, 3)
                            round_parts(1, 7)
                        ins = nc.scalar.activation(neg[:, k % SR, :, b], srcb[:, q % 2, :], ACT.Sign,
                                                   bias=dcol[:, layer, c:c + 1])
                    ins.then_inc(signs, 1)
                    if layer == 0 and done is not None and k == KB - 1:
                        copy_turned(done[1])
                    if layer == 0 and is_last(q):
                        if k == 1:
                            exps_of_d(1, 0, EARLY, 1)
                        if k >= 2:
                            round_parts(1, k - 2)
                    if layer == 1 and is_first(q):
                        if k == 0:
                            exps_of_d(1, EARLY, EARLY + NB, 2)
                        if k == 1:
                            round_parts(1, 6)
                    if done is not None and done[0] == 1 and k == 5:
                        elu(done[1])
                if layer == 1 and is_first(q):
                    exps_of_s(1)

            exps_of_d(0, 0, KB * NB, 0)
            exps_of_s(0)
            all_supertiles(act, body)
            elu(NQ - 1)

        @block.vector
        def _(dve):
            def encode(q, k):
                dve.wait_ge(adj_landed[k % 2], 16 * (4 * q + k // 2 + 1))
                if later(KB * q + k - 1):
                    dve.wait_ge(turned, KB * q + k - 1)
                apart(dve, q)
                nc.vector.tensor_scalar(enc8[:, k % 2, 0:VCOLS], adj_in[:, k % 2, 0:VCOLS], 0.0, float(NO_EDGE),
                                        ALU.is_gt, ALU.add).then_inc(enc_vec, 1)

            def extract(q, k):
                dve.wait_ge(turned, KB * q + k + 1)
                apart(dve, q)
                half = 4 * (k % 2)
                nc.vector.tensor_scalar(mask_t[:, q, half:half + 4, k // 2, :], tb[:, :, :].bitcast(U32),
                                        0x01010101, 6, ALU.bitwise_and, ALU.logical_shift_left).then_inc(masked, 1)

            def over_rows(a):
                return a.unsqueeze(1).broadcast_to([P, NQ * TI, F])

            def find_max(layer, chunks):
                nc.vector.tensor_reduce(stat[:, 0:1], dcol[:, layer, 0:chunks], AX.X, ALU.max).then_inc(stat_set, 1)

            def spread_max(layer):
                dve.wait_ge(stat_turned, layer + 1)
                nc.vector.tensor_reduce(gst[0:1, 0:1], pg[0:1, 0:P], AX.X, ALU.max).then_inc(gst_set, 1)

            def centre(layer, c0, c1):
                dve.wait_ge(cmax_set, layer + 1)
                nc.vector.tensor_scalar(dcen[:, c0:c1], dcol[:, layer, c0:c1], cmax[:, layer, 0:1], None,
                                        ALU.subtract).then_inc(dcen_set, 1)

            def take_max(layer):
                dve.wait_ge(max_spread, layer + 1)
                nc.vector.tensor_copy(cmax[:, layer, 0:1], pg[:, P:P + 1]).then_inc(cmax_set, 1)

            def clip_s(layer):
                flat = scol[:, layer, :, :].rearrange("p q t -> p (q t)")
                nc.vector.tensor_scalar(scen[:, 0, :], flat, cmax[:, layer, 0:1], 0.0, ALU.add, ALU.min)\
                    .then_inc(scen_set, 1)
                nc.vector.tensor_scalar(scen[:, 1, :], flat, cmax[:, layer, 0:1], 0.0, ALU.add, ALU.max)\
                    .then_inc(scen_set, 1)

            def set_scur(Q, layer, q):
                if later(Q):
                    dve.wait_ge(spread, Q)
                nc.vector.tensor_copy(scur[:, :], scol[:, layer, q, :]).then_inc(scur_set, 1)

            def weigh(layer, g):
                n = NQ * layer + g
                cs = slice(NB * g, NB * g + NB)
                w = weighed(layer, NB * g, NB * g + NB)
                for side in range(2):
                    if later(n):
                        dve.wait_ge(w_vec, WEIGH_V * n)
                    nc.vector.tensor_tensor(prod[:, side, :, :], val[:, cs, :], bcol[:, side, cs].unsqueeze(2)
                                            .broadcast_to([P, NB, FD]), ALU.mult).then_inc(w_vec, 1)
                for side in range(2):
                    dve.wait_ge(w_act, WEIGH_A * n + side + 1)
                    nc.vector.tensor_tensor(prod[:, side, :, :], prod[:, side, :, :],
                                            w[:, :, side * WC:side * WC + FD], ALU.subtract).then_inc(w_vec, 1)
                for side in range(2):
                    c = side * WC + FD
                    dve.wait_ge(w_act, WEIGH_A * n + 2 + side + 1)
                    nc.vector.tensor_tensor(w[:, :, c + FD:c + 2 * FD], prod[:, side, :, :], w[:, :, c:c + FD],
                                            ALU.subtract).then_inc(w_vec, 1)

            def negative(layer, q, k):
                u = KB * (NQ * layer + q) + k
                bits = mask_t[:, q, k, :, :].rearrange("p t i -> p (t i)").bitcast(U16)
                dve.wait_ge(signs, u + 1)
                if layer == 0 and k == 0:
                    dve.wait_ge(masked, KB * (q + 1))
                nc.vector.tensor_tensor(neg16[:, k % SR, :], neg16[:, k % SR, :], bits, ALU.bitwise_and)\
                    .then_inc(negs, 1)

            def positive(layer, q, k):
                u = KB * (NQ * layer + q) + k
                bits = mask_t[:, q, k, :, :].rearrange("p t i -> p (t i)").bitcast(U16)
                if later(u - MR + 1):
                    dve.wait_ge(mm_done, u - MR + 1)
                dve.wait_ge(negs, u + 1)
                nc.vector.tensor_tensor(pos16[:, k % MR, :], neg16[:, k % SR, :], bits, ALU.bitwise_xor)\
                    .then_inc(poss, 1)

            def sum_parts(layer, q, Q):
                if layer == 1 and is_first(q):
                    dve.wait_ge(pdone[0], EPI[0] * NQ)
                elif later(q):
                    dve.wait_ge(pdone[layer], EPI[layer] * q)
                for t in range(TI):
                    if t < TI - 1:
                        dve.wait_ge(acc_ready, (TI - 1) * Q + t + 1)
                    else:
                        dve.wait_ge(mm_done, KB * (Q + 1))
                    nc.vector.tensor_reduce(
                        part[:, t, :, :],
                        acc[t][:, 0:2 * WC].rearrange("p (s r c) -> p s c r", s=2, r=SPLIT),
                        AX.X, ALU.add).then_inc(acc_free, 1)

            def take_reciprocal(layer, q):
                dve.wait_ge(pdone[layer], EPI[layer] * q + 5)
                nc.vector.reciprocal(rden, den).then_inc(recips, 1)

            def take_stats(layer, q, Q):
                dve.wait_ge(pdone[layer], EPI[layer] * (q + 1) - 4)
                for t in range(TI):
                    nc.vector.bn_stats(bst[:, t, :], num[:, t, 0:F]).then_inc(bn_part, 1)
                dve.wait_ge(bn_part, TI * (Q + 1))
                apart(dve, q)
                for t in range(TI):
                    nc.vector.bn_aggr(mv[:, t, :], bst[:, t, :]).then_inc(bn_done, 1)

            def group_values(g):
                dve.wait_ge(projected, g + 1)
                v = pg[:, 0:NB * FD].rearrange("p (b c) -> p b c", c=FD)
                vv = val[:, :, :].rearrange("p (g b) c -> p g b c", b=NB)
                dd = dcol[:, 1, :].rearrange("p (g b) -> p g b", b=NB)
                nc.vector.tensor_copy(vv[:, g, :, 0:F], v[:, :, 0:F]).then_inc(grp_set, 1)
                nc.vector.tensor_copy(dd[:, g, :], v[:, :, F]).then_inc(grp_set, 1)
                nc.vector.tensor_copy(scol[:, 1, g, :], pg[:, NB * FD:NB * FD + TI]).then_inc(grp_set, 1)

            def sum_values():
                nc.vector.tensor_reduce(meanv[:, :], val[:, :, 0:F].rearrange("p c f -> p f c"), AX.X, ALU.add)\
                    .then_inc(mean_sum, 1)

            def take_mean(layer):
                dve.wait_ge(mean_ps, layer + 1)
                nc.vector.tensor_scalar(meanv[:, :], pg[:, 0:F], 1.0 / N, None, ALU.mult).then_inc(mean_set, 1)

            dve.wait_ge(w_landed, 16 * 4)
            dve.wait_ge(x_landed, 16)
            nc.vector.tensor_tensor(s_prod, x_all, over_rows(att0[:, 0, :]), ALU.mult).then_inc(s_mult, 1)
            encode(0, 0)
            dve.wait_ge(s_mult, 1)
            nc.vector.tensor_reduce(scol[:, 0, :, :].rearrange("p q t -> p (q t)"), s_prod, AX.X, ALU.add)\
                .then_inc(s_set, 1)
            dve.wait_ge(val_landed, 16 * KB)
            nc.vector.tensor_tensor(d_prod, val[:, :, 0:F], over_rows(att0[:, 1, :]), ALU.mult).then_inc(d_mult, 1)
            encode(0, 1)
            dve.wait_ge(d_mult, 1)
            nc.vector.tensor_reduce(dcol[:, 0, :], d_prod, AX.X, ALU.add).then_inc(d_set, 1)
            dve.wait_ge(s_set, 1)
            set_scur(0, 0, 0)
            dve.wait_ge(d_set, 1)
            find_max(0, KB * NB)
            extract(0, 0)
            nc.vector.tensor_copy(proj[:, 0:F], wl1[:, 0:F]).then_inc(proj_set, 1)
            dve.wait_ge(wa_ready, 1)
            nc.vector.tensor_copy(proj[:, F:F + 1], pg[0:F, F + 1:F + 2]).then_inc(proj_set, 1)
            nc.vector.tensor_copy(proj[:, F + 1:F + 2], pg[0:F, F:F + 1]).then_inc(proj_set, 1)
            encode(0, 2)
            spread_max(0)
            extract(0, 1)
            take_max(0)
            centre(0, 0, KB * NB)
            clip_s(0)
            for k in range(2, KB):
                if k < KB - 1:
                    encode(0, k + 1)
                extract(0, k)
            dve.wait_ge(b_set, 2)

            def body(layer, q):
                Q = NQ * layer + q
                prep, done = prepares(layer, q), before(layer, q)
                for k in range(KB):
                    if layer == 0 and is_first(q):
                        weigh(0, k)
                    if prep and k == 0:
                        encode(q + 1, 0)
                    if layer == 1 and is_first(q) and k == KB - 1:
                        group_values(NQ - 1)
                        dve.wait_ge(grp_set, 3 * NQ)
                        centre(1, EARLY + NB, EARLY + 2 * NB)
                        clip_s(1)
                        dve.wait_ge(b_set, 8)
                        weigh(1, 7)
                    if done is not None:
                        if k == 3:
                            take_reciprocal(*done[0:2])
                        if k == (5 if done[0] == 0 else 7):
                            take_stats(*done)
                    negative(layer, q, k)
                    if prep and k < KB - 1:
                        encode(q + 1, k + 1)
                    positive(layer, q, k)
                    if done is not None and k == 0:
                        sum_parts(*done)
                    if prep:
                        extract(q + 1, k)
                    if done is not None:
                        if layer == 0 and k == 7:
                            group_values(done[1])
                    if k == 2:
                        if not is_last(q):
                            set_scur(Q + 1, layer, q + 1)
                        elif layer == 0:
                            set_scur(NQ, 1, 0)
                    if layer == 0 and is_first(q):
                        if k == 5:
                            sum_values()
                        if k == 7:
                            take_mean(0)
                    if layer == 0 and is_last(q):
                        if k == 0:
                            dve.wait_ge(grp_set, 3 * (NQ - 2))
                            find_max(1, EARLY)
                        if k == 1:
                            spread_max(1)
                            take_max(1)
                            centre(1, 0, EARLY)
                            dve.wait_ge(b_set, 4)
                            dve.wait_ge(turned, KB * NQ)
                        if 2 <= k:
                            weigh(1, k - 2)
                    if layer == 1 and is_first(q):
                        if k == 0:
                            dve.wait_ge(grp_set, 3 * (NQ - 1))
                            centre(1, EARLY, EARLY + NB)
                        if k == 1:
                            dve.wait_ge(b_set, 6)
                            weigh(1, 6)
                        if k == 7:
                            sum_values()
                            take_mean(1)

            all_supertiles(dve, body)
            last = (1, NQ - 1, 2 * NQ - 1)
            sum_parts(*last)
            take_reciprocal(*last[0:2])
            take_stats(*last)

        @block.tensor
        def _(pe):
            pe.wait_ge(ident_set, 1)
            pe.wait_ge(w_landed, 16 * 4)
            nc.tensor.transpose(pg[0:F, 0:F], wl1[:, 0:F], ident[0:F, 0:F]).then_inc(wt_turned, 1)
            pe.wait_ge(wt_copied, 1)
            nc.tensor.matmul(pg[0:F, F:F + 2], wl1[:, F:2 * F], att1[:, :], start=True, stop=True)\
                .then_inc(wa_ready, 1)

            def turn_masks(q, k):
                n = KB * q + k
                pe.wait_ge(enc_vec, n + 1)
                pe.wait_ge(enc_pool, n + 1)
                if later(n):
                    pe.wait_ge(masked, n)
                for j in range(4):
                    ins = nc.tensor.transpose(tb[:, j, :], enc[:, k % 2, j * P:(j + 1) * P], ident[:, :])
                ins.then_inc(turned, 1)

            def spread_rows(Q, bank):
                pe.wait_ge(scur_set, Q + 1)
                if later(Q - 1):
                    pe.wait_ge(signs, KB * (Q - 1))
                for t in range(TI):
                    ins = nc.tensor.matmul(srcb[:, bank, t * P:(t + 1) * P], scur[:, t:t + 1].broadcast_to([P, P]),
                                           ident[:, :], start=True, stop=True)
                ins.then_inc(spread, 1)

            def turn_stat(layer):
                pe.wait_ge(stat_set, layer + 1)
                nc.tensor.transpose(pg[0:1, 0:P], stat[:, 0:1], ident[:, :]).then_inc(stat_turned, 1)

            def spread_stat(layer):
                pe.wait_ge(gst_set, layer + 1)
                nc.tensor.matmul(pg[:, P:P + 1], ones[0:1, :], gst[0:1, 0:1], start=True, stop=True)\
                    .then_inc(max_spread, 1)

            def turn_group(g):
                pe.wait_ge(pdone[0], EPI[0] * (g + 1))
                pe.wait_ge(mean_set, 1)
                if later(g):
                    pe.wait_ge(grp_set, 3 * g)
                if is_last(g):
                    pe.wait_ge(cmax_set, 2)
                apart(pe, g)
                for t in range(TI):
                    ins = nc.tensor.transpose(pg[0:F, t * P:(t + 1) * P], xout[:, t, :], ident[:, :])
                ins.then_inc(rows_turned, 1)

            def project_group(g):
                pe.wait_ge(xt_set, g + 1)
                pe.wait_ge(proj_set, 3)
                for b in range(NB):
                    nc.tensor.matmul(pg[:, b * FD:(b + 1) * FD], xt[:, b:ROWS:NB], proj[:, 0:FD],
                                     start=True, stop=True)
                for t in range(TI):
                    c = NB * FD + t
                    ins = nc.tensor.matmul(pg[:, c:c + 1], xt[:, t * P:(t + 1) * P], proj[:, FD:FD + 1],
                                           start=True, stop=True)
                ins.then_inc(projected, 1)

            def products(layer, q, k):
                Q = NQ * layer + q
                u = KB * Q + k
                pe.wait_ge(negs, u + 1)
                pe.wait_ge(poss, u + 1)
                apart(pe, q)
                if is_first(q):
                    pe.wait_ge(w_vec, WEIGH_V * (NQ * layer + k + 1))
                for t in range(TI):
                    if k == 0 and later(Q):
                        pe.wait_ge(acc_free, TI * (Q - 1) + t + 1)
                        apart(pe, q)
                    for b in range(NB):
                        c = NB * k + b
                        w = weighed(layer, c, c + 1)
                        for side, m in enumerate((pos8[:, k % MR], neg8[:, k % SR])):
                            first = k == 0 and b == 0 and side == 0
                            last = k == KB - 1 and b == NB - 1 and side == 1
                            ins = nc.tensor.matmul(
                                acc[t][:, side * WC:(side + 1) * WC], m[:, t * P:(t + 1) * P, b],
                                w[:, 0, side * WC:(side + 1) * WC], start=first, stop=last, skip_group_check=True)
                    if k == KB - 1 and t < TI - 1:
                        ins.then_inc(acc_ready, 1)
                ins.then_inc(mm_done, 1)

            def spread_mean(layer):
                pe.wait_ge(mean_sum, layer + 1)
                if layer == 0:
                    pe.wait_ge(cmax_set, 1)
                else:
                    pe.wait_ge(grp_set, 3 * NQ)
                nc.tensor.matmul(pg[:, 0:F], ones[:, :], meanv[:, :], start=True, stop=True).then_inc(mean_ps, 1)

            pe.wait_ge(ones_set, 2)
            turn_masks(0, 0)
            spread_rows(0, 0)
            pe.wait_ge(proj_set, 3)
            turn_stat(0)
            turn_masks(0, 1)
            spread_stat(0)
            for k in range(2, KB):
                turn_masks(0, k)

            def body(layer, q):
                Q = NQ * layer + q
                prep, done = prepares(layer, q), before(layer, q)
                for k in range(KB):
                    if prep:
                        turn_masks(q + 1, k)
                    if layer == 0 and done is not None:
                        if k == 6:
                            turn_group(done[1])
                        if k == 7:
                            project_group(done[1])
                    if layer == 0 and is_first(q) and k == 6:
                        spread_mean(0)
                    if layer == 0 and is_last(q) and k == 1:
                        pe.wait_ge(grp_set, 3 * (NQ - 2))
                        turn_stat(1)
                        spread_stat(1)
                    if layer == 1 and is_first(q):
                        if k == 5:
                            turn_group(NQ - 1)
                        if k == 6:
                            project_group(NQ - 1)
                    if k == 3:
                        if not is_last(q):
                            spread_rows(Q + 1, (q + 1) % 2)
                        elif layer == 0:
                            spread_rows(NQ, 0)
                    products(layer, q, k)
                if layer == 1 and is_first(q):
                    spread_mean(1)

            all_supertiles(pe, body)


def program(nc, x, adj, a0, w1, a1, x1_dram, out):
    fast_attention(nc, x, adj, a0, w1, a1, x1_dram, out)


def kernel(x, adj, L0_gnn_a, L1_gnn_W, L1_gnn_a):
    import numpy as _np
    import concourse.bacc as _bacc
    from concourse import mybir as _mybir
    from concourse.bass_utils import run_bass_kernel_spmd as _run

    nc = _bacc.Bacc("TRN2", target_bir_lowering=False, num_devices=1)
    arrays, args = {}, []
    for name, a in (("x", x), ("adj", adj), ("a0", L0_gnn_a), ("w1", L1_gnn_W), ("a1", L1_gnn_a)):
        a = _np.ascontiguousarray(a)
        arrays[f"in_{name}"] = a
        args.append(nc.dram_tensor(f"in_{name}", a.shape, _mybir.dt.from_np(a.dtype), kind="ExternalInput").ap())
    args.append(nc.dram_tensor("x1_rows", (N, F), F32, kind="Internal").ap())
    args.append(nc.dram_tensor("out_0", (N, F), F32, kind="ExternalOutput").ap())
    program(nc, *args)
    r = _run(nc, [arrays], core_ids=[0])
    return r.results[0]["out_0"]
```

```python
from contextlib import ExitStack

import concourse.bass as bass
from concourse import mybir

P = 128
N = 4096
F = 64
NQ = 8
TI = 4
KB = 8
NB = 4
ROWS = TI * P
UNIT = TI * N // KB
LEAD = 2
FD = F + 1
SPLIT = 3
WC = SPLIT * FD
SR = 4
MR = 2
SLOPE = (0.01, 0.2)
EPS = 1e-5
BELOW, ABOVE = -40.0, 20.0
LEAST = 1e-30
NO_EDGE = 0x30
EPI = (13, 17)
EARLY = 6
WEIGH = 4

ALU = mybir.AluOpType
ACT = mybir.ActivationFunctionType
AX = mybir.AxisListType
F32 = mybir.dt.float32
BF16 = mybir.dt.bfloat16
FP8 = mybir.dt.float8e4
I32 = mybir.dt.int32
U32 = mybir.dt.uint32
U16 = mybir.dt.uint16
U8 = mybir.dt.uint8
I8 = mybir.dt.int8


def fast_attention(nc, x, adj, a0, w1, a1, x1_dram, out, flag):
    with ExitStack() as ctx:
        def sb(name, shape, dt):
            return ctx.enter_context(nc.sbuf_tensor(name, shape, dt))

        def ps(name, shape, dt):
            return ctx.enter_context(nc.psum_tensor(name, shape, dt))

        def sem(name):
            return ctx.enter_context(nc.semaphore(name))

        mask_t = sb("mask_t", [P, NQ, KB, TI, P], U32)
        adj_in = sb("adj_in", [P, 4, UNIT // 2], I32)
        enc = sb("enc", [P, 2, UNIT // NB], F32)
        neg = sb("neg", [P, SR, ROWS, NB], I8)
        pos = sb("pos", [P, MR, ROWS, NB], I8)
        wmov = sb("wmov", [P, KB * NB, 2 * WC], BF16)
        val = sb("val", [P, KB * NB, FD], F32)
        prod = sb("prod", [P, 2, NB, FD], F32)
        xt = sb("xt", [F, ROWS], F32)
        scr = sb("scr", [P, 2, 2 * TI * FD], F32)
        resid = sb("resid", [P, TI, F], F32)
        xout = sb("xout", [P, TI, F], F32)
        ident = sb("ident", [P, P], F32)
        ones = sb("ones", [P, P], F32)
        half_col = sb("half_col", [P, 1], F32)
        att0 = sb("att0", [P, 2, F], F32)
        att1 = sb("att1", [F, 2], F32)
        wl1 = sb("wl1", [F, 2 * F], F32)
        proj = sb("proj", [F, F + 2], F32)
        dcol = sb("dcol", [P, 2, KB * NB], F32)
        scol = sb("scol", [P, 2, NQ, TI], F32)
        scur = sb("scur", [P, TI], F32)
        dcen = sb("dcen", [P, KB * NB], F32)
        scen = sb("scen", [P, 2, NQ * TI], F32)
        bcol = sb("bcol", [P, 2, KB * NB], F32)
        acol = sb("acol", [P, 2, 2, NQ, TI], F32)
        stat = sb("stat", [P, 2], F32)
        gst = sb("gst", [2, 4], F32)
        lim = sb("lim", [P, 2, 2], F32)
        ok = sb("ok", [P, 2], F32)
        cmax = sb("cmax", [P, 2, 2], F32)
        meanv = sb("meanv", [P, F], F32)
        small = sb("small", [P, 6, TI], F32)
        bst = sb("bst", [P, TI, 6], F32)
        mv = sb("mv", [P, TI, 2], F32)

        def spare(q, half):
            flat = mask_t[:, q, :, :, :].rearrange("p k t i -> p (k t i)").bitcast(F32)
            return flat[:, half * NQ * TI * F:(half + 1) * NQ * TI * F].rearrange("p (t d) -> p t d", d=F)

        x_all, s_prod, d_prod, x_chunks = (spare(NQ - 1, 0), spare(NQ - 1, 1), spare(NQ - 2, 0),
                                           spare(NQ - 2, 1))

        acc = [ps(f"acc{t}", [P, 512], F32) for t in range(TI)]
        tb = ps("tb", [P, TI, P], F32)
        pg = ps("pg", [P, 512], F32)
        srcb = ps("srcb", [P, 2, 512], F32)

        x_first = sem("x_first")
        x_landed = sem("x_landed")
        val_landed = sem("val_landed")
        val_set = sem("val_set")
        a_landed = sem("a_landed")
        w_landed = sem("w_landed")
        adj_landed = [sem(f"adj_landed{i}") for i in range(4)]
        res_landed = sem("res_landed")
        stored = sem("stored")
        ones_set = sem("ones_set")
        ident_zero = sem("ident_zero")
        ident_set = sem("ident_set")
        ones_col = sem("ones_col")
        wt_turned = sem("wt_turned")
        wt_copied = sem("wt_copied")
        wa_ready = sem("wa_ready")
        proj_set = sem("proj_set")
        s_first = sem("s_first")
        s_mult = sem("s_mult")
        d_mult = sem("d_mult")
        s_set = sem("s_set")
        d_set = sem("d_set")
        enc_vec = sem("enc_vec")
        enc_act = sem("enc_act")
        turned = sem("turned")
        masked = sem("masked")
        rows_turned = sem("rows_turned")
        xt_set = sem("xt_set")
        projected = sem("projected")
        grp_set = sem("grp_set")
        scur_set = sem("scur_set")
        spread = sem("spread")
        stat_set = sem("stat_set")
        stat_turned = sem("stat_turned")
        gst_set = sem("gst_set")
        max_spread = sem("max_spread")
        cmax_set = sem("cmax_set")
        dcen_set = sem("dcen_set")
        b_set = sem("b_set")
        scen_set = sem("scen_set")
        a_set = sem("a_set")
        w_prod = sem("w_prod")
        w_vec = sem("w_vec")
        w_act = sem("w_act")
        limits = sem("limits")
        ok_set = sem("ok_set")
        ok_turned = sem("ok_turned")
        flag_set = sem("flag_set")
        mean_sum = sem("mean_sum")
        mean_ps = sem("mean_ps")
        mean_set = sem("mean_set")
        signs = sem("signs")
        negs = sem("negs")
        poss = sem("poss")
        mm_done = sem("mm_done")
        acc_ready = sem("acc_ready")
        acc_free = sem("acc_free")
        pdone = [sem(f"pdone{i}") for i in range(2)]
        recips = sem("recips")
        bn_part = sem("bn_part")
        bn_done = sem("bn_done")
        elu_exp = sem("elu_exp")

        adj_v = adj.rearrange("(q h t p) (k j) -> q k h p t j", h=2, t=TI // 2, p=P, k=KB)
        x_rows = x.rearrange("(t p) d -> p t d", p=P)
        x_v = x.rearrange("(q t p) d -> q p t d", t=TI, p=P)
        x1_v = x1_dram.rearrange("(q t p) d -> q p t d", t=TI, p=P)
        out_v = out.rearrange("(q t p) d -> q p t d", t=TI, p=P)

        enc8 = enc[:, :, :].bitcast(U8)
        enc_signs = enc[:, :, :].bitcast(FP8)
        neg16 = neg[:, :, :, :].rearrange("p r i b -> p r (i b)").bitcast(U16)
        pos16 = pos[:, :, :, :].rearrange("p r i b -> p r (i b)").bitcast(U16)
        neg8 = neg[:, :, :, :].bitcast(FP8)
        pos8 = pos[:, :, :, :].bitcast(FP8)
        part = scr[:, 0, :].rearrange("p (t s c) -> p t s c", t=TI, s=2)
        num = scr[:, 1, 0:TI * FD].rearrange("p (t c) -> p t c", t=TI)
        tmp = scr[:, 1, TI * FD:2 * TI * FD].rearrange("p (t c) -> p t c", t=TI)
        zero_row, den, rden, var, rstd, mhalf = (small[:, i, :] for i in range(6))

        def wide(col, c):
            return col.unsqueeze(2).broadcast_to([P, TI, c])

        def later(count):
            return not isinstance(count, int) or count > 0

        def apart(eng, count):
            if not isinstance(count, int):
                eng.nop(nofuse=True)

        def is_first(q):
            return isinstance(q, int) and q == 0

        def is_last(q):
            return isinstance(q, int) and q == NQ - 1

        def all_supertiles(eng, body):
            for layer in range(2):
                body(layer, 0)
                with eng.Fori(0, (NQ - 2) // 2) as i:
                    body(layer, 2 * i + 1)
                    body(layer, 2 * i + 2)
                body(layer, NQ - 1)

        def ahead(layer, q, k, steps):
            if layer == 1 or is_last(q) and k + steps >= KB:
                return None
            return q + (k + steps) // KB, (k + steps) % KB

        def before(layer, q):
            if is_first(q):
                return None if layer == 0 else (0, NQ - 1, NQ - 1)
            return layer, q - 1, NQ * layer + q - 1

        def multiply(eng, ops, layer, g):
            n = NQ * layer + g
            cs = slice(NB * g, NB * g + NB)
            if layer == 1:
                eng.wait_ge(grp_set, 3 * (g + 1))
                eng.wait_ge(b_set, 4 if g < EARLY else 2 * (g - EARLY) + 6)
                eng.wait_ge(mm_done, KB * (NQ - 1) + g + 1)
            for side in range(2):
                if later(n):
                    eng.wait_ge(w_vec, WEIGH * n)
                ops.tensor_tensor(prod[:, side, :, :], val[:, cs, :], bcol[:, side, cs].unsqueeze(2)
                                  .broadcast_to([P, NB, FD]), ALU.mult).then_inc(w_prod, 1)

        def epilogue_sums(eng, ops, layer, q, Q):
            done, base = pdone[layer], EPI[layer] * q
            numf, tmpf = num[:, :, 0:F], tmp[:, :, 0:F]
            eng.wait_ge(acc_free, TI * (Q + 1))
            eng.wait_ge(a_set, 2 * (layer + 1))
            ops.tensor_tensor(num, part[:, :, 0, :], wide(acol[:, layer, 0, q, :], FD), ALU.mult)\
                .then_inc(done, 1)
            ops.tensor_tensor(tmp, part[:, :, 1, :], wide(acol[:, layer, 1, q, :], FD), ALU.mult)\
                .then_inc(done, 1)
            eng.wait_ge(done, base + 2)
            ops.tensor_tensor(num, num, tmp, ALU.add).then_inc(done, 1)

        def epilogue_empty_rows(eng, ops, layer, q, Q):
            done, base = pdone[layer], EPI[layer] * q
            numf, tmpf = num[:, :, 0:F], tmp[:, :, 0:F]
            eng.wait_ge(done, base + 3)
            apart(eng, q)
            ops.tensor_scalar(zero_row, num[:, :, F], LEAST, None, ALU.is_lt).then_inc(done, 1)
            eng.wait_ge(done, base + 4)
            ops.tensor_tensor(den, num[:, :, F], zero_row, ALU.add).then_inc(done, 1)
            eng.wait_ge(mean_set, layer + 1)
            ops.tensor_tensor(tmpf, wide(zero_row, F), meanv[:, :].unsqueeze(1)
                                    .broadcast_to([P, TI, F]), ALU.mult).then_inc(done, 1)
            eng.wait_ge(done, base + 6)
            ops.tensor_tensor(numf, numf, tmpf, ALU.add).then_inc(done, 1)

        def epilogue_divide(eng, ops, layer, q, Q):
            done, base = pdone[layer], EPI[layer] * q
            numf, tmpf = num[:, :, 0:F], tmp[:, :, 0:F]
            eng.wait_ge(recips, Q + 1)
            eng.wait_ge(done, base + 7)
            ops.tensor_tensor(numf, numf, wide(rden, F), ALU.mult).then_inc(done, 1)
            eng.wait_ge(done, base + 8)
            if layer == 1:
                apart(eng, q)
                ops.tensor_scalar(tmpf, numf, 0.0, None, ALU.min).then_inc(done, 1)
                eng.wait_ge(done, base + 9)
                apart(eng, q)
                ops.tensor_scalar(numf, numf, 0.0, None, ALU.max).then_inc(done, 1)
                eng.wait_ge(elu_exp, q + 1)
                apart(eng, q)
                ops.tensor_scalar(tmpf, tmpf, -1.0, None, ALU.add).then_inc(done, 1)
                eng.wait_ge(done, base + 11)
                ops.tensor_tensor(numf, numf, tmpf, ALU.add).then_inc(done, 1)
                eng.wait_ge(done, base + 12)
            eng.wait_ge(res_landed, 16 * (Q + 1))
            ops.tensor_tensor(numf, numf, resid[:, :, :], ALU.add).then_inc(done, 1)

        def epilogue_norm(eng, ops, layer, q, Q):
            done, end = pdone[layer], EPI[layer] * (q + 1)
            numf = num[:, :, 0:F]
            eng.wait_ge(bn_done, TI * (Q + 1))
            apart(eng, q)
            ops.tensor_scalar(var, mv[:, :, 1], EPS, None, ALU.add).then_inc(done, 1)
            eng.wait_ge(done, end - 3)
            if ops is nc.gpsimd:
                ops.tensor_tensor(rstd, var, mhalf, ALU.pow).then_inc(done, 1)
            ops.tensor_tensor(numf, numf, wide(mv[:, :, 0], F), ALU.subtract).then_inc(done, 1)

        def epilogue_end(eng, ops, layer, q, Q):
            done, end = pdone[layer], EPI[layer] * (q + 1)
            numf = num[:, :, 0:F]
            eng.wait_ge(done, end - 1)
            if later(Q):
                eng.wait_ge(stored, 16 * Q)
            if layer == 1:
                eng.wait_ge(rows_turned, NQ)
            elif later(q):
                eng.wait_ge(rows_turned, q)
            ops.tensor_tensor(xout[:, :, :], numf, wide(rstd, F), ALU.mult).then_inc(done, 1)

        block = ctx.enter_context(nc.Block())

        @block.sync
        def _(sp):
            sp.dma_start(att0[:, :, :], a0.rearrange("(s d) o -> o s d", s=2).partition_broadcast(P)
                         .rearrange("p o s d -> p (o s) d")).then_inc(a_landed, 16)

            def load_adj(q, k):
                for half in range(2):
                    if later(KB * q + k - 1):
                        sp.wait_ge(enc_vec, 2 * (KB * q + k - 2) + half + 1)
                        apart(sp, q)
                        if half == 1:
                            sp.wait_ge(enc_act, KB * q + k - 1)
                            apart(sp, q)
                    slot = 2 * (k % 2) + half
                    sp.dma_start(adj_in[:, slot, :].rearrange("p (t j) -> p t j", t=TI // 2), adj_v[q, k, half])\
                        .then_inc(adj_landed[slot], 16)

            for half in range(2):
                sp.dma_start(att1[:, half:half + 1], a1[half * F:(half + 1) * F, :]).then_inc(w_landed, 16)
            sp.dma_start(wl1[:, 0:F], w1).then_inc(w_landed, 16)
            sp.wait_ge(val_landed, 16)
            load_adj(0, 0)
            load_adj(0, 1)
            load_adj(0, 2)

            def store(layer, q):
                sp.wait_ge(pdone[layer], EPI[layer] * (q + 1))
                sp.dma_start((x1_v if layer == 0 else out_v)[q], xout[:, :, :]).then_inc(stored, 16)

            def load_resid(layer, q):
                if layer == 1 and is_first(q):
                    sp.wait_ge(pdone[0], EPI[0] * NQ - 4)
                elif later(q):
                    sp.wait_ge(pdone[layer], EPI[layer] * q - 4)
                if layer == 1:
                    sp.wait_ge(stored, 16 * NQ)
                sp.dma_start(resid[:, :, :], (x_v if layer == 0 else x1_v)[q]).then_inc(res_landed, 16)

            def body(layer, q):
                for k in range(KB):
                    if ahead(layer, q, k, LEAD + 1):
                        load_adj(*ahead(layer, q, k, LEAD + 1))
                if layer == 0:
                    load_resid(0, q)
                if before(layer, q) is not None:
                    store(*before(layer, q)[0:2])
                if layer == 1:
                    load_resid(1, q)

            all_supertiles(sp, body)
            store(1, NQ - 1)
            sp.wait_ge(stored, 16 * 2 * NQ)

        @block.gpsimd
        def _(pool):
            nc.gpsimd.memset(ident[:, :], 0.0).then_inc(ident_zero, 1)
            nc.gpsimd.memset(half_col[:, :], 0.5).then_inc(ones_set, 1)
            nc.gpsimd.memset(ones[:, :], 1.0).then_inc(ones_set, 1)
            nc.gpsimd.memset(mhalf, -0.5).then_inc(ones_set, 1)
            pool.wait_ge(ident_zero, 1)
            nc.gpsimd.affine_select(out=ident[:, :], in_=ident[:, :], compare_op=ALU.not_equal, fill=1.0,
                                    base=0, pattern=[[-1, P]], channel_multiplier=1).then_inc(ident_set, 1)
            nc.gpsimd.memset(val[:, :, F:FD], 1.0).then_inc(ones_col, 1)
            pool.wait_ge(ones_set, 3)

            pool.wait_ge(val_set, 1)
            pool.wait_ge(ones_col, 1)
            pool.wait_ge(b_set, 2)
            multiply(pool, nc.gpsimd, 0, 0)
            pool.wait_ge(x_landed, 16)
            pool.wait_ge(a_landed, 16)
            nc.gpsimd.tensor_tensor(s_prod[:, TI:], x_all[:, TI:], att0[:, 0, :].unsqueeze(1)
                                    .broadcast_to([P, (NQ - 1) * TI, F]), ALU.mult).then_inc(s_mult, 1)
            for g in range(1, KB):
                multiply(pool, nc.gpsimd, 0, g)

            def body(layer, q):
                done = before(layer, q)
                stages = {0: epilogue_sums, 1: epilogue_empty_rows, 2: epilogue_divide, 4: epilogue_norm,
                          5: epilogue_end}
                groups = {}
                if layer == 0 and is_last(q):
                    groups = {6: (2, 3, 4)}
                if layer == 1 and is_first(q):
                    groups = {}
                for k in range(KB):
                    for g in groups.get(k, ()):
                        multiply(pool, nc.gpsimd, 1, g)
                    if done is not None and k in stages:
                        stages[k](pool, nc.gpsimd, *done)

            all_supertiles(pool, body)
            pool.wait_ge(pdone[1], EPI[1] * NQ - 3)
            nc.gpsimd.tensor_tensor(rstd, var, mhalf, ALU.pow).then_inc(pdone[1], 1)

        @block.scalar
        def _(act):
            act.dma_start(x_chunks.rearrange("p (k b) d -> p k (b d)", b=NB),
                          x.rearrange("(k p b) d -> p k (b d)", p=P, b=NB)).then_inc(val_landed, 16)
            act.dma_start(x_all[:, 0:TI], x_rows[:, 0:TI]).then_inc(x_first, 16)
            act.wait_ge(val_landed, 16)
            nc.scalar.copy(val[:, :, 0:F], x_chunks).then_inc(val_set, 1)
            act.dma_start(x_all[:, TI:], x_rows[:, TI:]).then_inc(x_landed, 16)
            act.wait_ge(wt_turned, 1)
            nc.scalar.copy(wl1[:, F:2 * F], pg[0:F, 0:F]).then_inc(wt_copied, 1)

            def encode_last(q, k):
                act.wait_ge(adj_landed[2 * (k % 2) + 1], 16 * (4 * q + k // 2 + 1))
                if later(KB * q + k - 1):
                    act.wait_ge(turned, KB * q + k - 1)
                apart(act, q)
                nc.scalar.activation(enc_signs[:, k % 2, (TI - 1) * UNIT // TI:], adj_in[:, 2 * (k % 2) + 1, UNIT // TI:],
                                     ACT.Sign, bias=half_col[:, :], scale=-1.0, saturate=False).then_inc(enc_act, 1)

            def exps_of_d(layer, c0, c1, n):
                act.wait_ge(dcen_set, n + 1)
                nc.scalar.activation(bcol[:, 0, c0:c1], dcen[:, c0:c1], ACT.Exp).then_inc(b_set, 1)
                nc.scalar.activation(bcol[:, 1, c0:c1], dcen[:, c0:c1], ACT.Exp, scale=SLOPE[layer])\
                    .then_inc(b_set, 1)

            def exps_of_s(layer):
                act.wait_ge(scen_set, 2 * (layer + 1))
                for side, scale in ((0, 1 - SLOPE[layer]), (1, SLOPE[layer] - 1)):
                    nc.scalar.activation(acol[:, layer, side, :, :].rearrange("p q t -> p (q t)"),
                                         scen[:, side, :], ACT.Exp, scale=scale).then_inc(a_set, 1)

            def round_parts(layer, g):
                w = wmov[:, NB * g:NB * g + NB]
                for lot in range(2):
                    for side in range(2):
                        c = side * WC + lot * FD
                        if lot == 0:
                            act.wait_ge(w_prod, 2 * (NQ * layer + g) + side + 1)
                        else:
                            act.wait_ge(w_vec, WEIGH * (NQ * layer + g) + side + 1)
                        nc.scalar.copy(w[:, :, c:c + FD], prod[:, side, :, :]).then_inc(w_act, 1)

            def elu(q):
                act.wait_ge(pdone[1], EPI[1] * q + 9)
                nc.scalar.activation(tmp[:, :, 0:F], tmp[:, :, 0:F], ACT.Exp).then_inc(elu_exp, 1)

            def body(layer, q):
                Q = NQ * layer + q
                done = before(layer, q)
                for k in range(KB):
                    u = KB * Q + k
                    if k == 0:
                        act.wait_ge(spread, Q + 1)
                    if later(u - SR + 1):
                        act.wait_ge(mm_done, u - SR + 1)
                    apart(act, q)
                    for b in range(NB):
                        c = NB * k + b
                        ins = nc.scalar.activation(neg[:, k % SR, :, b], srcb[:, q % 2, :], ACT.Sign,
                                                   bias=dcol[:, layer, c:c + 1])
                    ins.then_inc(signs, 1)
                    if ahead(layer, q, k, LEAD):
                        encode_last(*ahead(layer, q, k, LEAD))
                    if layer == 0 and is_first(q):
                        if k > 0:
                            round_parts(0, k)
                        if k == 3:
                            exps_of_s(0)
                    if layer == 0 and is_last(q):
                        if k == 2:
                            exps_of_d(1, 0, NB * EARLY, 1)
                        if k >= 4:
                            round_parts(1, k - 4)
                    if layer == 1 and is_first(q):
                        if k == 1:
                            exps_of_d(1, NB * EARLY, NB * (EARLY + 1), 2)
                        if k < 3:
                            round_parts(1, k + 4)
                        if k == 6:
                            exps_of_d(1, NB * (EARLY + 1), NB * KB, 3)
                        if k == 7:
                            round_parts(1, 7)
                    if done is not None and done[0] == 1 and k == 5:
                        elu(done[1])
                if layer == 1 and is_first(q):
                    exps_of_s(1)

            act.wait_ge(ones_set, 3)
            exps_of_d(0, 0, KB * NB, 0)
            encode_last(0, 0)
            round_parts(0, 0)
            encode_last(0, 1)
            all_supertiles(act, body)
            elu(NQ - 1)

        @block.vector
        def _(dve):
            def encode(q, k, half):
                slot = 2 * (k % 2) + half
                size = UNIT // 2 if half == 0 else UNIT // TI
                dve.wait_ge(adj_landed[slot], 16 * (4 * q + k // 2 + 1))
                if half == 0 and later(KB * q + k - 1):
                    dve.wait_ge(turned, KB * q + k - 1)
                apart(dve, q)
                nc.vector.tensor_scalar(enc8[:, k % 2, half * UNIT // 2:half * UNIT // 2 + size],
                                        adj_in[:, slot, 0:size], 0.0, float(NO_EDGE), ALU.is_gt, ALU.add)\
                    .then_inc(enc_vec, 1)

            def extract(q, k):
                dve.wait_ge(turned, KB * q + k + 1)
                apart(dve, q)
                nc.vector.tensor_scalar(mask_t[:, q, k, 0:TI - 1, :], tb[:, 0:TI - 1, :].bitcast(U32),
                                        0x01010101, 6, ALU.bitwise_and, ALU.logical_shift_left)
                nc.vector.tensor_scalar(mask_t[:, q, k, TI - 1, :], tb[:, TI - 1, :].bitcast(U32),
                                        0x80808080, 1, ALU.bitwise_and, ALU.logical_shift_right).then_inc(masked, 1)

            def over_rows(a, tiles):
                return a.unsqueeze(1).broadcast_to([P, tiles, F])

            def find_max(layer, chunks):
                nc.vector.tensor_reduce(stat[:, 0:1], dcol[:, layer, 0:chunks], AX.X, ALU.max).then_inc(stat_set, 1)

            def spread_max(layer):
                dve.wait_ge(stat_turned, layer + 1)
                nc.vector.tensor_reduce(gst[0:1, 0:1], pg[0:1, 0:P], AX.X, ALU.max).then_inc(gst_set, 1)

            def centre(layer, c0, c1):
                dve.wait_ge(cmax_set, layer + 1)
                nc.vector.tensor_scalar(dcen[:, c0:c1], dcol[:, layer, c0:c1], cmax[:, layer, 0:1], ABOVE,
                                        ALU.subtract, ALU.min).then_inc(dcen_set, 1)

            def take_max(layer):
                dve.wait_ge(max_spread, layer + 1)
                nc.vector.tensor_copy(cmax[:, layer, 0:1], pg[:, P:P + 1]).then_inc(cmax_set, 1)

            def clip_s(layer):
                flat = scol[:, layer, :, :].rearrange("p q t -> p (q t)")
                nc.vector.tensor_scalar(scen[:, 0, :], flat, cmax[:, layer, 0:1], 0.0, ALU.add, ALU.min)\
                    .then_inc(scen_set, 1)
                nc.vector.tensor_scalar(scen[:, 1, :], flat, cmax[:, layer, 0:1], 0.0, ALU.add, ALU.max)\
                    .then_inc(scen_set, 1)

            def set_scur(Q, layer, q):
                if later(Q):
                    dve.wait_ge(spread, Q)
                nc.vector.tensor_copy(scur[:, :], scol[:, layer, q, :]).then_inc(scur_set, 1)

            def weigh(layer, g):
                n = NQ * layer + g
                w = wmov[:, NB * g:NB * g + NB]
                for side in range(2):
                    dve.wait_ge(w_act, WEIGH * n + side + 1)
                    nc.vector.tensor_tensor(prod[:, side, :, :], prod[:, side, :, :],
                                            w[:, :, side * WC:side * WC + FD], ALU.subtract).then_inc(w_vec, 1)
                for side in range(2):
                    c = side * WC + FD
                    dve.wait_ge(w_act, WEIGH * n + 2 + side + 1)
                    nc.vector.tensor_tensor(w[:, :, c + FD:c + 2 * FD], prod[:, side, :, :], w[:, :, c:c + FD],
                                            ALU.subtract).then_inc(w_vec, 1)

            def negative(layer, q, k):
                u = KB * (NQ * layer + q) + k
                bits = mask_t[:, q, k, :, :].rearrange("p t i -> p (t i)").bitcast(U16)
                dve.wait_ge(signs, u + 1)
                if layer == 0:
                    dve.wait_ge(masked, u + 1)
                nc.vector.tensor_tensor(neg16[:, k % SR, :], neg16[:, k % SR, :], bits, ALU.bitwise_and)\
                    .then_inc(negs, 1)

            def positive(layer, q, k):
                u = KB * (NQ * layer + q) + k
                bits = mask_t[:, q, k, :, :].rearrange("p t i -> p (t i)").bitcast(U16)
                if later(u - MR + 1):
                    dve.wait_ge(mm_done, u - MR + 1)
                dve.wait_ge(negs, u + 1)
                nc.vector.tensor_tensor(pos16[:, k % MR, :], neg16[:, k % SR, :], bits, ALU.bitwise_xor)\
                    .then_inc(poss, 1)

            def sum_parts(layer, q, Q):
                if layer == 1 and is_first(q):
                    dve.wait_ge(pdone[0], EPI[0] * NQ)
                elif later(q):
                    dve.wait_ge(pdone[layer], EPI[layer] * q)
                for t in range(TI):
                    if t < TI - 1:
                        dve.wait_ge(acc_ready, (TI - 1) * Q + t + 1)
                    else:
                        dve.wait_ge(mm_done, KB * (Q + 1))
                    nc.vector.tensor_reduce(
                        part[:, t, :, :],
                        acc[t][:, 0:2 * WC].rearrange("p (s r c) -> p s c r", s=2, r=SPLIT),
                        AX.X, ALU.add).then_inc(acc_free, 1)

            def take_reciprocal(layer, q):
                dve.wait_ge(pdone[layer], EPI[layer] * q + 5)
                nc.vector.reciprocal(rden, den).then_inc(recips, 1)

            def take_stats(layer, q, Q):
                dve.wait_ge(pdone[layer], EPI[layer] * (q + 1) - 4)
                for t in range(TI):
                    nc.vector.bn_stats(bst[:, t, :], num[:, t, 0:F]).then_inc(bn_part, 1)
                dve.wait_ge(bn_part, TI * (Q + 1))
                apart(dve, q)
                for t in range(TI):
                    nc.vector.bn_aggr(mv[:, t, :], bst[:, t, :]).then_inc(bn_done, 1)

            def copy_turned(g):
                dve.wait_ge(rows_turned, g + 1)
                if later(g):
                    dve.wait_ge(projected, g)
                apart(dve, g)
                nc.vector.tensor_copy(xt[:, :], pg[0:F, :]).then_inc(xt_set, 1)

            def group_values(g):
                dve.wait_ge(projected, g + 1)
                v = pg[:, 0:NB * FD].rearrange("p (b c) -> p b c", c=FD)
                vv = val[:, :, :].rearrange("p (g b) c -> p g b c", b=NB)
                dd = dcol[:, 1, :].rearrange("p (g b) -> p g b", b=NB)
                nc.vector.tensor_copy(vv[:, g, :, 0:F], v[:, :, 0:F]).then_inc(grp_set, 1)
                nc.vector.tensor_copy(dd[:, g, :], v[:, :, F]).then_inc(grp_set, 1)
                nc.vector.tensor_copy(scol[:, 1, g, :], pg[:, NB * FD:NB * FD + TI]).then_inc(grp_set, 1)

            def sum_values():
                nc.vector.tensor_reduce(meanv[:, :], val[:, :, 0:F].rearrange("p c f -> p f c"), AX.X, ALU.add)\
                    .then_inc(mean_sum, 1)

            def find_limits(layer):
                dve.wait_ge(dcen_set, 4 if layer else 1)
                for i, op in enumerate((ALU.min, ALU.max)):
                    nc.vector.tensor_reduce(lim[:, i, layer:layer + 1], dcen[:, :], AX.X, op).then_inc(limits, 1)

            def judge():
                dve.wait_ge(limits, 4)
                nc.vector.tensor_scalar(lim[:, 0, :], lim[:, 0, :], BELOW, None, ALU.is_ge).then_inc(limits, 1)
                nc.vector.tensor_scalar(lim[:, 1, :], lim[:, 1, :], ABOVE, None, ALU.is_lt).then_inc(limits, 1)
                dve.wait_ge(limits, 6)
                nc.vector.tensor_reduce(ok[:, 0:1], lim[:, :, :].rearrange("p a b -> p (a b)"), AX.X, ALU.min)\
                    .then_inc(ok_set, 1)

            def set_flag():
                dve.wait_ge(ok_turned, 1)
                nc.vector.tensor_reduce(ok[0:1, 1:2], pg[0:1, P:2 * P], AX.X, ALU.min).then_inc(ok_set, 1)
                dve.wait_ge(ok_set, 2)
                nc.vector.tensor_scalar(flag[0:1, 0:1], ok[0:1, 1:2], 0.5, None, ALU.is_lt).then_inc(flag_set, 1)

            def take_mean(layer):
                dve.wait_ge(mean_ps, layer + 1)
                nc.vector.tensor_scalar(meanv[:, :], pg[:, 0:F], 1.0 / N, None, ALU.mult).then_inc(mean_set, 1)

            dve.wait_ge(a_landed, 16)
            dve.wait_ge(val_landed, 16)
            nc.vector.tensor_tensor(d_prod, x_chunks, over_rows(att0[:, 1, :], NQ * TI), ALU.mult)\
                .then_inc(d_mult, 1)
            dve.wait_ge(d_mult, 1)
            nc.vector.tensor_reduce(dcol[:, 0, :], d_prod, AX.X, ALU.add).then_inc(d_set, 1)
            dve.wait_ge(w_landed, 16 * 3)
            nc.vector.tensor_copy(proj[:, 0:F], wl1[:, 0:F]).then_inc(proj_set, 1)
            dve.wait_ge(wa_ready, 1)
            nc.vector.tensor_copy(proj[:, F:F + 1], pg[0:F, F + 1:F + 2]).then_inc(proj_set, 1)
            nc.vector.tensor_copy(proj[:, F + 1:F + 2], pg[0:F, F:F + 1]).then_inc(proj_set, 1)
            dve.wait_ge(d_set, 1)
            find_max(0, KB * NB)
            dve.wait_ge(x_first, 16)
            nc.vector.tensor_tensor(s_prod[:, 0:TI], x_all[:, 0:TI], over_rows(att0[:, 0, :], TI), ALU.mult)\
                .then_inc(s_first, 1)
            spread_max(0)
            dve.wait_ge(s_first, 1)
            nc.vector.tensor_reduce(scol[:, 0, 0, :], s_prod[:, 0:TI], AX.X, ALU.add).then_inc(s_set, 1)
            take_max(0)
            dve.wait_ge(s_set, 1)
            set_scur(0, 0, 0)
            centre(0, 0, KB * NB)
            encode(0, 0, 0)
            encode(0, 0, 1)
            weigh(0, 0)
            encode(0, 1, 0)
            encode(0, 1, 1)
            extract(0, 0)
            encode(0, 2, 0)
            encode(0, 2, 1)
            extract(0, 1)
            def body(layer, q):
                Q = NQ * layer + q
                done = before(layer, q)
                for k in range(KB):
                    if done is not None and done[0] == 0 and k == (KB - 1 if layer == 0 else 5):
                        copy_turned(done[1])
                    if done is not None:
                        if k == 3:
                            take_reciprocal(*done[0:2])
                        if k == 7 and done[0] == 1:
                            take_stats(*done)
                    if layer == 0 and is_first(q) and k > 0:
                        weigh(0, k)
                    negative(layer, q, k)
                    if ahead(layer, q, k, LEAD + 1):
                        encode(*ahead(layer, q, k, LEAD + 1), 0)
                    positive(layer, q, k)
                    if ahead(layer, q, k, LEAD + 1):
                        encode(*ahead(layer, q, k, LEAD + 1), 1)
                    if done is not None and k == 0:
                        sum_parts(*done)
                    if done is not None and done[0] == 0 and k == (4 if layer == 0 else 3):
                        take_stats(*done)
                    if layer == 1 and is_first(q) and k == 6:
                        group_values(NQ - 1)
                        dve.wait_ge(grp_set, 3 * NQ)
                        centre(1, NB * (EARLY + 1), NB * KB)
                        clip_s(1)
                        multiply(dve, nc.vector, 1, 7)
                        sum_values()
                        find_limits(1)
                        judge()
                        weigh(1, 7)
                    if ahead(layer, q, k, LEAD):
                        extract(*ahead(layer, q, k, LEAD))
                    if done is not None:
                        if layer == 0 and k == 7:
                            group_values(done[1])
                    if layer == 0 and is_first(q) and k == 2:
                        dve.wait_ge(s_mult, 1)
                        nc.vector.tensor_reduce(scol[:, 0, 1:, :].rearrange("p q t -> p (q t)"), s_prod[:, TI:],
                                                AX.X, ALU.add).then_inc(s_set, 1)
                        dve.wait_ge(s_set, 2)
                        clip_s(0)
                    if k == 2:
                        if not is_last(q):
                            set_scur(Q + 1, layer, q + 1)
                        elif layer == 0:
                            set_scur(NQ, 1, 0)
                    if layer == 0 and is_first(q):
                        if k == 5:
                            dve.wait_ge(val_set, 1)
                            sum_values()
                            find_limits(0)
                        if k == 7:
                            take_mean(0)
                    if layer == 0 and is_last(q):
                        if k == 0:
                            dve.wait_ge(grp_set, 3 * (NQ - 2))
                            find_max(1, NB * EARLY)
                        if k == 1:
                            spread_max(1)
                            take_max(1)
                            centre(1, 0, NB * EARLY)
                        if k in (3, 4):
                            multiply(dve, nc.vector, 1, k - 3)
                        if k >= 3:
                            weigh(1, k - 3)
                    if layer == 1 and is_first(q):
                        if k == 0:
                            dve.wait_ge(grp_set, 3 * (NQ - 1))
                            centre(1, NB * EARLY, NB * (EARLY + 1))
                            multiply(dve, nc.vector, 1, 5)
                            weigh(1, 5)
                        if k == 1:
                            multiply(dve, nc.vector, 1, 6)
                            weigh(1, 6)
                        if k == 7:
                            set_flag()
                            take_mean(1)

            all_supertiles(dve, body)
            last = (1, NQ - 1, 2 * NQ - 1)
            sum_parts(*last)
            epilogue_sums(dve, nc.vector, *last)
            epilogue_empty_rows(dve, nc.vector, *last)
            take_reciprocal(*last[0:2])
            epilogue_divide(dve, nc.vector, *last)
            take_stats(*last)
            epilogue_norm(dve, nc.vector, *last)
            epilogue_end(dve, nc.vector, *last)

        @block.tensor
        def _(pe):
            pe.wait_ge(ident_set, 1)
            pe.wait_ge(w_landed, 16 * 3)
            nc.tensor.transpose(pg[0:F, 0:F], wl1[:, 0:F], ident[0:F, 0:F]).then_inc(wt_turned, 1)
            pe.wait_ge(wt_copied, 1)
            nc.tensor.matmul(pg[0:F, F:F + 2], wl1[:, F:2 * F], att1[:, :], start=True, stop=True)\
                .then_inc(wa_ready, 1)

            def turn_masks(q, k):
                n = KB * q + k
                pe.wait_ge(enc_vec, 2 * (n + 1))
                pe.wait_ge(enc_act, n + 1)
                if later(n):
                    pe.wait_ge(masked, n)
                for t in range(TI):
                    ins = nc.tensor.transpose(tb[:, t, :], enc[:, k % 2, t * P:(t + 1) * P], ident[:, :])
                ins.then_inc(turned, 1)

            def spread_rows(Q, bank):
                pe.wait_ge(scur_set, Q + 1)
                if later(Q - 1):
                    pe.wait_ge(signs, KB * (Q - 1))
                for t in range(TI):
                    ins = nc.tensor.transpose(srcb[:, bank, t * P:(t + 1) * P], scur[:, t:t + 1].broadcast_to([P, P]),
                                              ident[:, :])
                ins.then_inc(spread, 1)

            def turn_stat(layer):
                pe.wait_ge(stat_set, layer + 1)
                nc.tensor.transpose(pg[0:1, 0:P], stat[:, 0:1], ident[:, :]).then_inc(stat_turned, 1)

            def spread_stat(layer):
                pe.wait_ge(gst_set, layer + 1)
                nc.tensor.matmul(pg[:, P:P + 1], ones[0:1, :], gst[0:1, 0:1], start=True, stop=True)\
                    .then_inc(max_spread, 1)

            def turn_group(g):
                pe.wait_ge(pdone[0], EPI[0] * (g + 1))
                pe.wait_ge(mean_set, 1)
                if later(g):
                    pe.wait_ge(grp_set, 3 * g)
                if is_last(g):
                    pe.wait_ge(cmax_set, 2)
                apart(pe, g)
                for t in range(TI):
                    ins = nc.tensor.transpose(pg[0:F, t * P:(t + 1) * P], xout[:, t, :], ident[:, :])
                ins.then_inc(rows_turned, 1)

            def project_group(g):
                pe.wait_ge(xt_set, g + 1)
                pe.wait_ge(proj_set, 3)
                for b in range(NB):
                    nc.tensor.matmul(pg[:, b * FD:(b + 1) * FD], xt[:, b:ROWS:NB], proj[:, 0:FD],
                                     start=True, stop=True)
                for t in range(TI):
                    c = NB * FD + t
                    ins = nc.tensor.matmul(pg[:, c:c + 1], xt[:, t * P:(t + 1) * P], proj[:, FD:FD + 1],
                                           start=True, stop=True)
                ins.then_inc(projected, 1)

            def products(layer, q, k):
                Q = NQ * layer + q
                u = KB * Q + k
                pe.wait_ge(poss, u + 1)
                apart(pe, q)
                if is_first(q):
                    pe.wait_ge(w_vec, WEIGH * (NQ * layer + k + 1))
                for t in range(TI):
                    if k == 0 and later(Q):
                        pe.wait_ge(acc_free, TI * (Q - 1) + t + 1)
                        apart(pe, q)
                    for b in range(NB):
                        c = NB * k + b
                        for side, m in enumerate((pos8[:, k % MR], neg8[:, k % SR])):
                            first = k == 0 and b == 0 and side == 0
                            last = k == KB - 1 and b == NB - 1 and side == 1
                            ins = nc.tensor.matmul(
                                acc[t][:, side * WC:(side + 1) * WC], m[:, t * P:(t + 1) * P, b],
                                wmov[:, c, side * WC:(side + 1) * WC], start=first, stop=last, skip_group_check=True)
                    if k == KB - 1 and t < TI - 1:
                        ins.then_inc(acc_ready, 1)
                ins.then_inc(mm_done, 1)

            def spread_mean(layer):
                pe.wait_ge(mean_sum, layer + 1)
                if layer == 0:
                    pe.wait_ge(cmax_set, 1)
                else:
                    pe.wait_ge(grp_set, 3 * NQ)
                nc.tensor.matmul(pg[:, 0:F], ones[:, :], meanv[:, :], start=True, stop=True).then_inc(mean_ps, 1)

            pe.wait_ge(ones_set, 3)
            pe.wait_ge(proj_set, 3)
            turn_stat(0)
            spread_stat(0)
            spread_rows(0, 0)
            turn_masks(0, 0)
            turn_masks(0, 1)

            def body(layer, q):
                Q = NQ * layer + q
                done = before(layer, q)
                for k in range(KB):
                    if ahead(layer, q, k, LEAD):
                        turn_masks(*ahead(layer, q, k, LEAD))
                    if layer == 0 and done is not None:
                        if k == 6:
                            turn_group(done[1])
                        if k == 7:
                            project_group(done[1])
                    if layer == 0 and is_first(q) and k == 6:
                        spread_mean(0)
                    if layer == 0 and is_last(q) and k == 1:
                        pe.wait_ge(grp_set, 3 * (NQ - 2))
                        turn_stat(1)
                        spread_stat(1)
                    if layer == 1 and is_first(q):
                        if k == 4:
                            turn_group(NQ - 1)
                        if k == 5:
                            project_group(NQ - 1)
                        if k == 7:
                            spread_mean(1)
                            pe.wait_ge(ok_set, 1)
                            nc.tensor.transpose(pg[0:1, P:2 * P], ok[:, 0:1], ident[:, :]).then_inc(ok_turned, 1)
                    if k == 3:
                        if not is_last(q):
                            spread_rows(Q + 1, (q + 1) % 2)
                        elif layer == 0:
                            spread_rows(NQ, 0)
                    products(layer, q, k)

            all_supertiles(pe, body)


def general_attention(nc, x, adj, a0, w1, a1, out):
    R = N // P
    G = R // TI
    NV = 10
    ROW_STEPS = (4, 8)

    with ExitStack() as ctx:
        def sb(name, shape, dt):
            return ctx.enter_context(nc.sbuf_tensor(name, shape, dt))

        def sem(name):
            return ctx.enter_context(nc.semaphore(name))

        xg = sb("g_x", [P, 2, R, F], F32)
        hg = sb("g_h", [P, R, F], F32)
        att = sb("g_att", [P, 2, 2, F], F32)
        wg = sb("g_w", [F, F], F32)
        ident = sb("g_ident", [P, P], F32)
        mhalf = sb("g_mhalf", [P, 1], F32)
        prod = sb("g_prod", [P, R, F], F32)
        s_col = sb("g_s", [P, R, 1], F32)
        d_col = sb("g_d", [P, R], F32)
        d_row = sb("g_d_row", [P, N], F32)
        adj_t = sb("g_adj", [P, N], I32)
        edge = sb("g_edge", [P, N], F32)
        e = sb("g_e", [P, N], F32)
        slope = sb("g_slope", [P, N], F32)
        pt = sb("g_pt", [P, 2, TI, P], F32)
        xc = sb("g_xc", [P, F], F32)
        xct = sb("g_xct", [F, P], F32)
        s_cur = sb("g_s_cur", [P, 1], F32)
        nmax = sb("g_nmax", [P, 1], F32)
        total = sb("g_total", [P, 1], F32)
        o = sb("g_o", [P, F], F32)
        low = sb("g_low", [P, F], F32)
        bst = sb("g_bst", [P, 6], F32)
        mv = sb("g_mv", [P, 2], F32)
        var = sb("g_var", [P, 1], F32)
        rstd = sb("g_rstd", [P, 1], F32)
        spread_ps = ctx.enter_context(nc.psum_tensor("g_spread_ps", [P, TI, P], F32))
        turn_ps = ctx.enter_context(nc.psum_tensor("g_turn_ps", [P, 2, TI, P], F32))
        sum_ps = ctx.enter_context(nc.psum_tensor("g_sum_ps", [P, F], F32))
        xct_ps = ctx.enter_context(nc.psum_tensor("g_xct_ps", [F, P], F32))
        h_ps = ctx.enter_context(nc.psum_tensor("g_h_ps", [P, F], F32))

        landed = sem("g_landed")
        ident_zero = sem("g_ident_zero")
        constants = sem("g_constants")
        chunk_copied = sem("g_chunk_copied")
        chunk_turned = sem("g_chunk_turned")
        turned_copied = sem("g_turned_copied")
        chunk_projected = sem("g_chunk_projected")
        values_set = sem("g_values_set")
        products_set = sem("g_products_set")
        sd_set = sem("g_sd_set")
        d_spread = sem("g_d_spread")
        d_row_set = sem("g_d_row_set")
        adj_landed = sem("g_adj_landed")
        steps = sem("g_steps")
        exps = sem("g_exps")
        total_set = sem("g_total_set")
        w_turned = sem("g_w_turned")
        w_copied = sem("g_w_copied")
        rows_summed = sem("g_rows_summed")
        rows_done = [sem(f"g_rows_done{i}") for i in range(2)]
        low_exp = sem("g_low_exp")
        var_set = sem("g_var_set")
        rstd_set = sem("g_rstd_set")
        tile_done = sem("g_tile_done")
        stored = sem("g_stored")

        def values(layer):
            return hg[:, :, :] if layer else xg[:, 0]

        def apart(eng, count):
            if not isinstance(count, int):
                eng.nop(nofuse=True)

        block = ctx.enter_context(nc.Block())

        @block.sync
        def _(sp):
            sp.dma_start(xg[:, 0], x.rearrange("(t p) d -> p t d", p=P)).then_inc(landed, 16)
            for layer, a in enumerate((a0, a1)):
                sp.dma_start(att[:, layer], a.rearrange("(s d) o -> o s d", s=2).partition_broadcast(P)
                             .rearrange("p o s d -> p (o s) d")).then_inc(landed, 16)
            sp.dma_start(wg[:, :], w1).then_inc(landed, 16)
            for layer in range(2):
                def row_tile(r):
                    n = R * layer + r
                    if not isinstance(n, int) or n > 0:
                        sp.wait_ge(tile_done, n)
                    sp.dma_start(adj_t[:, :], adj.rearrange("(t p) j -> t p j", p=P)[r]).then_inc(adj_landed, 16)
                    if layer == 1:
                        sp.wait_ge(tile_done, n + 1)
                        sp.dma_start(out.rearrange("(t p) d -> t p d", p=P)[r], o[:, :]).then_inc(stored, 16)
                row_tile(0)
                with sp.Fori(1, R) as r:
                    row_tile(r)
            sp.wait_ge(stored, 16 * R)

        @block.gpsimd
        def _(pool):
            nc.gpsimd.memset(ident[:, :], 0.0).then_inc(ident_zero, 1)
            nc.gpsimd.memset(mhalf[:, :], -0.5).then_inc(constants, 1)
            pool.wait_ge(ident_zero, 1)
            nc.gpsimd.affine_select(out=ident[:, :], in_=ident[:, :], compare_op=ALU.not_equal, fill=1.0,
                                    base=0, pattern=[[-1, P]], channel_multiplier=1).then_inc(constants, 1)
            pool.wait_ge(constants, 2)
            with pool.Fori(0, 2 * R) as n:
                pool.wait_ge(var_set, n + 1)
                nc.gpsimd.tensor_tensor(rstd[:, :], var[:, :], mhalf[:, :], ALU.pow).then_inc(rstd_set, 1)

        @block.scalar
        def _(act):
            for layer in range(2):
                with act.Fori(0, R) as r:
                    n = R * layer + r
                    act.wait_ge(steps, NV * n + NV)
                    act.nop(nofuse=True)
                    nc.scalar.activation(e[:, :], e[:, :], ACT.Exp, bias=nmax[:, :]).then_inc(exps, 1)
                    if layer == 1:
                        act.wait_ge(rows_done[1], ROW_STEPS[1] * r + 2)
                        nc.scalar.activation(low[:, :], low[:, :], ACT.Exp).then_inc(low_exp, 1)

        @block.tensor
        def _(pe):
            pe.wait_ge(constants, 2)
            pe.wait_ge(landed, 16 * 4)
            for layer in range(2):
                if layer == 1:
                    with pe.Fori(0, R) as c:
                        pe.wait_ge(chunk_copied, c + 1)
                        pe.nop(nofuse=True)
                        nc.tensor.transpose(xct_ps[:, :], xc[:, :], ident[:, :]).then_inc(chunk_turned, 1)
                        pe.wait_ge(turned_copied, c + 1)
                        pe.nop(nofuse=True)
                        nc.tensor.matmul(h_ps[:, :], xct[:, :], wg[:, :], start=True, stop=True)\
                            .then_inc(chunk_projected, 1)
                pe.wait_ge(sd_set, 2 * layer + 2)
                for g in range(G):
                    if layer or g:
                        pe.wait_ge(d_row_set, G * layer + g)
                    for t in range(TI):
                        c = TI * g + t
                        ins = nc.tensor.matmul(spread_ps[:, t, :], d_col[:, c:c + 1].broadcast_to([P, P]), ident[:, :],
                                               start=True, stop=True)
                    ins.then_inc(d_spread, 1)
                with pe.Fori(0, R) as r:
                    n = R * layer + r
                    pe.wait_ge(exps, n + 1)
                    pe.nop(nofuse=True)

                    def turn(g):
                        if g >= 2:
                            pe.wait_ge(w_copied, G * n + g - 1)
                            pe.nop(nofuse=True)
                        for t in range(TI):
                            c = TI * g + t
                            ins = nc.tensor.transpose(turn_ps[:, g % 2, t, :], e[:, c * P:(c + 1) * P], ident[:, :])
                        ins.then_inc(w_turned, 1)

                    turn(0)
                    for g in range(G):
                        if g < G - 1:
                            turn(g + 1)
                        pe.wait_ge(w_copied, G * n + g + 1)
                        pe.nop(nofuse=True)
                        for t in range(TI):
                            c = TI * g + t
                            ins = nc.tensor.matmul(sum_ps[:, :], pt[:, g % 2, t, :], values(layer)[:, c, :],
                                                   start=c == 0, stop=c == R - 1)
                        ins.then_inc(rows_summed, 1)

        @block.vector
        def _(dve):
            dve.wait_ge(landed, 16 * 4)
            for layer in range(2):
                if layer == 1:
                    with dve.Fori(0, R) as c:
                        nc.vector.tensor_copy(xc[:, :], xg[:, 1, c, :]).then_inc(chunk_copied, 1)
                        dve.wait_ge(chunk_turned, c + 1)
                        nc.vector.tensor_copy(xct[:, :], xct_ps[:, :]).then_inc(turned_copied, 1)
                        dve.wait_ge(chunk_projected, c + 1)
                        nc.vector.tensor_copy(hg[:, c, :], h_ps[:, :]).then_inc(values_set, 1)
                    dve.wait_ge(values_set, R)
                for side, col in enumerate((s_col[:, :, 0], d_col[:, :])):
                    if layer or side:
                        dve.wait_ge(sd_set, 2 * layer + side)
                    nc.vector.tensor_tensor(prod[:, :, :], values(layer)[:, :, :], att[:, layer, side].unsqueeze(1)
                                            .broadcast_to([P, R, F]), ALU.mult).then_inc(products_set, 1)
                    dve.wait_ge(products_set, 2 * layer + side + 1)
                    nc.vector.tensor_reduce(col, prod[:, :, :], AX.X, ALU.add).then_inc(sd_set, 1)
                for g in range(G):
                    dve.wait_ge(d_spread, G * layer + g + 1)
                    nc.vector.tensor_copy(d_row[:, g * TI * P:(g + 1) * TI * P],
                                          spread_ps[:, :, :].rearrange("p t i -> p (t i)")).then_inc(d_row_set, 1)
                dve.wait_ge(d_row_set, G * (layer + 1))
                dve.wait_ge(sd_set, 2 * layer + 2)

                def row_tile(r):
                    n = R * layer + r
                    base = NV * n
                    nc.vector.tensor_copy(s_cur[:, :], s_col[:, r, :]).then_inc(steps, 1)
                    dve.wait_ge(steps, base + 1)
                    apart(dve, r)
                    nc.vector.tensor_scalar(e[:, :], d_row[:, :], s_cur[:, 0:1], None, ALU.add).then_inc(steps, 1)
                    dve.wait_ge(steps, base + 2)
                    apart(dve, r)
                    nc.vector.tensor_scalar(slope[:, :], e[:, :], SLOPE[layer], None, ALU.mult).then_inc(steps, 1)
                    dve.wait_ge(steps, base + 3)
                    nc.vector.tensor_tensor(e[:, :], e[:, :], slope[:, :], ALU.max).then_inc(steps, 1)
                    dve.wait_ge(adj_landed, 16 * (n + 1))
                    apart(dve, r)
                    nc.vector.tensor_scalar(edge[:, :], adj_t[:, :], 0.0, None, ALU.is_gt).then_inc(steps, 1)
                    dve.wait_ge(steps, base + 5)
                    nc.vector.tensor_tensor(e[:, :], e[:, :], edge[:, :], ALU.mult).then_inc(steps, 1)
                    nc.vector.tensor_scalar(slope[:, :], edge[:, :], -1.0, 9e15, ALU.add, ALU.mult).then_inc(steps, 1)
                    dve.wait_ge(steps, base + 7)
                    nc.vector.tensor_tensor(e[:, :], e[:, :], slope[:, :], ALU.add).then_inc(steps, 1)
                    dve.wait_ge(steps, base + 8)
                    nc.vector.tensor_reduce(nmax[:, :], e[:, :], AX.X, ALU.max).then_inc(steps, 1)
                    dve.wait_ge(steps, base + 9)
                    apart(dve, r)
                    nc.vector.tensor_scalar(nmax[:, :], nmax[:, :], -1.0, None, ALU.mult).then_inc(steps, 1)
                    dve.wait_ge(exps, n + 1)
                    nc.vector.tensor_reduce(total[:, :], e[:, :], AX.X, ALU.add).then_inc(total_set, 1)
                    dve.wait_ge(total_set, 2 * n + 1)
                    nc.vector.reciprocal(total[:, :], total[:, :]).then_inc(total_set, 1)
                    for g in range(G):
                        if g >= 2:
                            dve.wait_ge(rows_summed, G * n + g - 1)
                            apart(dve, r)
                        dve.wait_ge(w_turned, G * n + g + 1)
                        nc.vector.tensor_copy(pt[:, g % 2], turn_ps[:, g % 2]).then_inc(w_copied, 1)
                    done, row = rows_done[layer], ROW_STEPS[layer] * r
                    dve.wait_ge(total_set, 2 * n + 2)
                    apart(dve, r)
                    dve.wait_ge(rows_summed, G * (n + 1))
                    apart(dve, r)
                    if layer == 1 and not (isinstance(r, int) and r == 0):
                        dve.wait_ge(stored, 16 * r)
                        apart(dve, r)
                    nc.vector.tensor_scalar(o[:, :], sum_ps[:, :], total[:, 0:1], None, ALU.mult).then_inc(done, 1)
                    dve.wait_ge(done, row + 1)
                    apart(dve, r)
                    if layer == 1:
                        nc.vector.tensor_scalar(low[:, :], o[:, :], 0.0, None, ALU.min).then_inc(done, 1)
                        dve.wait_ge(done, row + 2)
                        apart(dve, r)
                        nc.vector.tensor_scalar(o[:, :], o[:, :], 0.0, None, ALU.max).then_inc(done, 1)
                        dve.wait_ge(low_exp, r + 1)
                        apart(dve, r)
                        nc.vector.tensor_scalar(low[:, :], low[:, :], -1.0, None, ALU.add).then_inc(done, 1)
                        dve.wait_ge(done, row + 4)
                        nc.vector.tensor_tensor(o[:, :], o[:, :], low[:, :], ALU.add).then_inc(done, 1)
                        dve.wait_ge(done, row + 5)
                    nc.vector.tensor_tensor(o[:, :], o[:, :], xg[:, layer, r, :], ALU.add).then_inc(done, 1)
                    dve.wait_ge(done, row + ROW_STEPS[layer] - 2)
                    nc.vector.bn_stats(bst[:, :], o[:, :]).then_inc(done, 1)
                    dve.wait_ge(done, row + ROW_STEPS[layer] - 1)
                    apart(dve, r)
                    nc.vector.bn_aggr(mv[:, :], bst[:, :]).then_inc(done, 1)
                    dve.wait_ge(done, row + ROW_STEPS[layer])
                    apart(dve, r)
                    nc.vector.tensor_scalar(var[:, :], mv[:, 1:2], EPS, None, ALU.add).then_inc(var_set, 1)
                    dve.wait_ge(rstd_set, n + 1)
                    apart(dve, r)
                    nc.vector.tensor_scalar(o[:, :] if layer else xg[:, 1, r, :], o[:, :], mv[:, 0:1], rstd[:, 0:1],
                                            ALU.subtract, ALU.mult).then_inc(tile_done, 1)

                row_tile(0)
                with dve.Fori(1, R) as r:
                    row_tile(r)
                dve.wait_ge(tile_done, R * (layer + 1))


def program(nc, x, adj, a0, w1, a1, x1_dram, out):
    with nc.sbuf_tensor("spread_flag", [1, 1], I32) as flag:
        fast_attention(nc, x, adj, a0, w1, a1, x1_dram, out, flag)
        too_far = nc.values_load(flag[0:1, 0:1], min_val=0, max_val=1)
        with nc.If(too_far > 0):
            general_attention(nc, x, adj, a0, w1, a1, out)


def kernel(x, adj, L0_gnn_a, L1_gnn_W, L1_gnn_a):
    import numpy as _np
    import concourse.bacc as _bacc
    from concourse import mybir as _mybir
    from concourse.bass_utils import run_bass_kernel_spmd as _run

    nc = _bacc.Bacc("TRN2", target_bir_lowering=False, num_devices=1)
    arrays, args = {}, []
    for name, a in (("x", x), ("adj", adj), ("a0", L0_gnn_a), ("w1", L1_gnn_W), ("a1", L1_gnn_a)):
        a = _np.ascontiguousarray(a)
        arrays[f"in_{name}"] = a
        args.append(nc.dram_tensor(f"in_{name}", a.shape, _mybir.dt.from_np(a.dtype), kind="ExternalInput").ap())
    args.append(nc.dram_tensor("x1_rows", (N, F), F32, kind="Internal").ap())
    args.append(nc.dram_tensor("out_0", (N, F), F32, kind="ExternalOutput").ap())
    program(nc, *args)
    r = _run(nc, [arrays], core_ids=[0])
    return r.results[0]["out_0"]
```
